# Optimizing a Trainium2 kernel written in Bass

```python
import numpy as np
import jax
import jax.numpy as jnp

def _softmax(x, axis=-1):
    return jax.nn.softmax(x, axis=axis)

def _gelu(x):
    return jax.nn.gelu(x, approximate=True)

def _silu(x):
    return jax.nn.silu(x)

def _sigmoid(x):
    return jax.nn.sigmoid(x)

def _layernorm(x, axis=-1, eps=1e-05):
    m = jnp.mean(x, axis=axis, keepdims=True)
    v = jnp.var(x, axis=axis, keepdims=True)
    return (x - m) / jnp.sqrt(v + eps)

def _scatter_add(tgt, idx, src, axis=0):
    return tgt.at[idx].add(src)

def _segment_sum(src, seg, n):
    return jax.ops.segment_sum(src, seg, n)
kernel_name = 'mk_gnn_resnorm_d4_gnn_r8_d2a9d0'

def setup_inputs(seed: int=0):
    np.random.seed(seed)
    _w = jnp.asarray

    def _rec_inputs():
        import jax
        import jax.numpy as jnp
        _gk = jax.random.key(seed)
        x = -0.0005207 + 1.001 * jax.random.normal(jax.random.fold_in(_gk, 1), (512, 512), jnp.float32)
        src = jax.random.randint(jax.random.fold_in(_gk, 2), (16384,), 0, 512, jnp.int32)
        dst = jnp.minimum((512 * jax.random.uniform(jax.random.fold_in(_gk, 3), (16384,)) ** 2.0).astype(jnp.int32), 4095)
        _o = jnp.argsort(dst, stable=True)
        src = src[_o]
        dst = dst[_o]
        edge_weight = jax.random.uniform(jax.random.fold_in(_gk, 12), (16384,), jnp.float32, 0.0, 0.999996)
        return (x, src, dst, edge_weight)
    x, src, dst, edge_weight = _rec_inputs()

    def _L0_gnn_setup():
        import jax, jax.numpy as jnp
        import numpy as np
        EMBED_DIM = 512
        NUM_HEADS = 8
        HEAD_DIM = EMBED_DIM // NUM_HEADS
        N = 512
        E = 16384
        EPS = 1e-05
        NEG = -1000000000.0

        def layer_norm(x, g, b):
            mu = jnp.mean(x, axis=-1, keepdims=True)
            var = jnp.mean(jnp.square(x - mu), axis=-1, keepdims=True)
            return (x - mu) * jax.lax.rsqrt(var + EPS) * g + b
        key = jax.random.key(seed)
        ks = jax.random.split(key, 12)
        D = EMBED_DIM
        s = 1.0 / np.sqrt(D)
        return {'x': jax.random.normal(ks[0], (N, D), jnp.float32), 'edge_index': jax.random.randint(ks[1], (2, E), 0, N, jnp.int64), 'edge_weight': jax.random.uniform(ks[2], (E,), jnp.float32), 'Wqkv': jax.random.normal(ks[3], (3 * D, D), jnp.float32) * s, 'bqkv': jnp.zeros((3 * D,), jnp.float32), 'Wo': jax.random.normal(ks[4], (D, D), jnp.float32) * s, 'bo': jnp.zeros((D,), jnp.float32), 'W1': jax.random.normal(ks[5], (D, D), jnp.float32) * s, 'b1': jnp.zeros((D,), jnp.float32), 'g1': jnp.ones((D,), jnp.float32), 'beta1': jnp.zeros((D,), jnp.float32), 'g2': jnp.ones((D,), jnp.float32), 'beta2': jnp.zeros((D,), jnp.float32)}
    _L0_gnn_all = _L0_gnn_setup()
    _L0_gnn_in = {k: v for k, v in _L0_gnn_all.items() if k in ('Wqkv', 'bqkv', 'Wo', 'bo', 'W1', 'b1', 'g1', 'beta1', 'g2', 'beta2')}
    del _L0_gnn_all

    def _L1_gnn_setup():
        import jax, jax.numpy as jnp
        import numpy as np
        N = 6250
        IN_CH = 512
        OUT_CH = 512
        DEG = 32
        E = N * DEG
        key = jax.random.key(seed)
        kx, kwc, kwn, kb, ke = jax.random.split(key, 5)
        x = jax.random.normal(kx, (N, IN_CH), dtype=jnp.float32)
        bound = 1.0 / np.sqrt(IN_CH)
        wc = jax.random.uniform(kwc, (IN_CH, OUT_CH), minval=-bound, maxval=bound, dtype=jnp.float32)
        wn = jax.random.uniform(kwn, (IN_CH, OUT_CH), minval=-bound, maxval=bound, dtype=jnp.float32)
        bias = jax.random.uniform(kb, (OUT_CH,), minval=-bound, maxval=bound, dtype=jnp.float32)
        src = jnp.repeat(jnp.arange(N, dtype=jnp.int64), DEG)
        dst = jax.random.randint(ke, (E,), 0, N, dtype=jnp.int64)
        edge_index = jnp.stack([src, dst], axis=0)
        return {'x': x, 'wc': wc, 'wn': wn, 'bias': bias, 'edge_index': edge_index}
    _L1_gnn_all = _L1_gnn_setup()
    _L1_gnn_in = {k: v for k, v in _L1_gnn_all.items() if k in ('wc', 'wn', 'bias')}
    del _L1_gnn_all

    def _L2_gnn_setup():
        import jax, jax.numpy as jnp
        import numpy as np
        N, E = (512, 16384)
        D_IN, D_OUT, H = (512, 512, 8)
        HEAD = D_OUT // H
        EPS = 1e-05

        def _layer_norm(x, g, b):
            m = jnp.mean(x, axis=-1, keepdims=True)
            v = jnp.mean(jnp.square(x - m), axis=-1, keepdims=True)
            return (x - m) * jax.lax.rsqrt(v + EPS) * g + b
        key = jax.random.key(seed)
        ks = jax.random.split(key, 16)
        s = 1.0 / np.sqrt(D_OUT)
        inp = {'x': jax.random.normal(ks[0], (N, D_IN), dtype=jnp.float32), 'edge_index': jax.random.randint(ks[1], (2, E), 0, N, dtype=jnp.int64), 'Wq': jax.random.normal(ks[2], (D_OUT, D_OUT), jnp.float32) * s, 'bq': jnp.zeros((D_OUT,), jnp.float32), 'Wk': jax.random.normal(ks[3], (D_OUT, D_OUT), jnp.float32) * s, 'bk': jnp.zeros((D_OUT,), jnp.float32), 'Wv': jax.random.normal(ks[4], (D_OUT, D_OUT), jnp.float32) * s, 'bv': jnp.zeros((D_OUT,), jnp.float32), 'Wo': jax.random.normal(ks[5], (D_OUT, D_OUT), jnp.float32) * s, 'bo': jnp.zeros((D_OUT,), jnp.float32), 'W1': jax.random.normal(ks[6], (D_OUT, 2 * D_OUT), jnp.float32) * s, 'b1': jnp.zeros((2 * D_OUT,), jnp.float32), 'W2': jax.random.normal(ks[7], (2 * D_OUT, D_OUT), jnp.float32) * (1.0 / np.sqrt(2 * D_OUT)), 'b2': jnp.zeros((D_OUT,), jnp.float32), 'g1': jnp.ones((D_OUT,), jnp.float32), 'be1': jnp.zeros((D_OUT,), jnp.float32), 'g2': jnp.ones((D_OUT,), jnp.float32), 'be2': jnp.zeros((D_OUT,), jnp.float32)}
        return inp
    _L2_gnn_all = _L2_gnn_setup()
    _L2_gnn_in = {k: v for k, v in _L2_gnn_all.items() if k in ('Wq', 'bq', 'Wk', 'bk', 'Wv', 'bv', 'Wo', 'bo', 'W1', 'b1', 'W2', 'b2', 'g1', 'be1', 'g2', 'be2')}
    del _L2_gnn_all

    def _L3_gnn_setup():
        import jax, jax.numpy as jnp
        import numpy as np
        N_NODES = 6250
        IN_CH = 512
        OUT_CH = 512
        N_EDGES = 100000
        key = jax.random.key(seed)
        k_x, k_e, k_w, k_b = jax.random.split(key, 4)
        x = jax.random.normal(k_x, (N_NODES, IN_CH), dtype=jnp.float32)
        edge_index = jax.random.randint(k_e, (2, N_EDGES), 0, N_NODES, dtype=jnp.int32)
        bound = 1.0 / np.sqrt(2 * IN_CH)
        W = jax.random.uniform(k_w, (OUT_CH, 2 * IN_CH), minval=-bound, maxval=bound, dtype=jnp.float32)
        b = jax.random.uniform(k_b, (OUT_CH,), minval=-bound, maxval=bound, dtype=jnp.float32)
        return {'x': x, 'edge_index': edge_index, 'W': W, 'b': b}
    _L3_gnn_all = _L3_gnn_setup()
    _L3_gnn_in = {k: v for k, v in _L3_gnn_all.items() if k in ('W', 'b')}
    del _L3_gnn_all
    return {'x': x, 'src': src, 'dst': dst, 'edge_weight': edge_weight, 'L0_gnn_Wqkv': _L0_gnn_in['Wqkv'], 'L0_gnn_bqkv': _L0_gnn_in['bqkv'], 'L0_gnn_Wo': _L0_gnn_in['Wo'], 'L0_gnn_bo': _L0_gnn_in['bo'], 'L0_gnn_W1': _L0_gnn_in['W1'], 'L0_gnn_b1': _L0_gnn_in['b1'], 'L0_gnn_g1': _L0_gnn_in['g1'], 'L0_gnn_beta1': _L0_gnn_in['beta1'], 'L0_gnn_g2': _L0_gnn_in['g2'], 'L0_gnn_beta2': _L0_gnn_in['beta2'], 'L1_gnn_wc': _L1_gnn_in['wc'], 'L1_gnn_wn': _L1_gnn_in['wn'], 'L1_gnn_bias': _L1_gnn_in['bias'], 'L2_gnn_Wq': _L2_gnn_in['Wq'], 'L2_gnn_bq': _L2_gnn_in['bq'], 'L2_gnn_Wk': _L2_gnn_in['Wk'], 'L2_gnn_bk': _L2_gnn_in['bk'], 'L2_gnn_Wv': _L2_gnn_in['Wv'], 'L2_gnn_bv': _L2_gnn_in['bv'], 'L2_gnn_Wo': _L2_gnn_in['Wo'], 'L2_gnn_bo': _L2_gnn_in['bo'], 'L2_gnn_W1': _L2_gnn_in['W1'], 'L2_gnn_b1': _L2_gnn_in['b1'], 'L2_gnn_W2': _L2_gnn_in['W2'], 'L2_gnn_b2': _L2_gnn_in['b2'], 'L2_gnn_g1': _L2_gnn_in['g1'], 'L2_gnn_be1': _L2_gnn_in['be1'], 'L2_gnn_g2': _L2_gnn_in['g2'], 'L2_gnn_be2': _L2_gnn_in['be2'], 'L3_gnn_W': _L3_gnn_in['W'], 'L3_gnn_b': _L3_gnn_in['b']}

def reference(x, src, dst, edge_weight, L0_gnn_Wqkv, L0_gnn_bqkv, L0_gnn_Wo, L0_gnn_bo, L0_gnn_W1, L0_gnn_b1, L0_gnn_g1, L0_gnn_beta1, L0_gnn_g2, L0_gnn_beta2, L1_gnn_wc, L1_gnn_wn, L1_gnn_bias, L2_gnn_Wq, L2_gnn_bq, L2_gnn_Wk, L2_gnn_bk, L2_gnn_Wv, L2_gnn_bv, L2_gnn_Wo, L2_gnn_bo, L2_gnn_W1, L2_gnn_b1, L2_gnn_W2, L2_gnn_b2, L2_gnn_g1, L2_gnn_be1, L2_gnn_g2, L2_gnn_be2, L3_gnn_W, L3_gnn_b):
    import jax
    import jax.numpy as jnp

    def _L0_gnn_ref(x, edge_index, edge_weight, Wqkv, bqkv, Wo, bo, W1, b1, g1, beta1, g2, beta2):
        import jax, jax.numpy as jnp
        import numpy as np
        EMBED_DIM = 512
        NUM_HEADS = 8
        HEAD_DIM = EMBED_DIM // NUM_HEADS
        N = 512
        E = 16384
        EPS = 1e-05
        NEG = -1000000000.0

        def layer_norm(x, g, b):
            mu = jnp.mean(x, axis=-1, keepdims=True)
            var = jnp.mean(jnp.square(x - mu), axis=-1, keepdims=True)
            return (x - mu) * jax.lax.rsqrt(var + EPS) * g + b
        n = x.shape[0]
        src, dst = (edge_index[0], edge_index[1])
        diag = jnp.arange(n)
        bias = jnp.full((n, n), NEG, dtype=x.dtype)
        bias = bias.at[diag, diag].set(0.0)
        bias = bias.at[dst, src].set(edge_weight.astype(x.dtype))
        qkv = x @ Wqkv.T + bqkv
        q, k, v = jnp.split(qkv, 3, axis=-1)
        q = q.reshape(n, NUM_HEADS, HEAD_DIM).transpose(1, 0, 2)
        k = k.reshape(n, NUM_HEADS, HEAD_DIM).transpose(1, 0, 2)
        v = v.reshape(n, NUM_HEADS, HEAD_DIM).transpose(1, 0, 2)
        scores = jnp.einsum('hnd,hmd->hnm', q, k) / np.sqrt(HEAD_DIM)
        scores = scores + bias[None, :, :]
        attn = jax.nn.softmax(scores, axis=-1)
        out = jnp.einsum('hnm,hmd->hnd', attn, v)
        out = out.transpose(1, 0, 2).reshape(n, EMBED_DIM)
        attn_out = out @ Wo.T + bo
        h = layer_norm(x + attn_out, g1, beta1)
        h = layer_norm(h + (h @ W1.T + b1), g2, beta2)
        return h

    def _L1_gnn_ref(x, wc, wn, bias, edge_index):
        import jax, jax.numpy as jnp
        import numpy as np
        N = 6250
        IN_CH = 512
        OUT_CH = 512
        DEG = 32
        E = N * DEG
        alpha = x @ wc
        beta = x @ wn
        src, dst = (edge_index[0], edge_index[1])
        sums = jax.ops.segment_sum(beta[dst], src, num_segments=x.shape[0])
        counts = jax.ops.segment_sum(jnp.ones_like(src, dtype=beta.dtype), src, num_segments=x.shape[0])
        gamma = sums / counts[:, None]
        return alpha + gamma + bias

    def _L2_gnn_ref(x, edge_index, Wq, bq, Wk, bk, Wv, bv, Wo, bo, W1, b1, W2, b2, g1, be1, g2, be2):
        import jax, jax.numpy as jnp
        import numpy as np
        N, E = (512, 16384)
        D_IN, D_OUT, H = (512, 512, 8)
        HEAD = D_OUT // H
        EPS = 1e-05

        def _layer_norm(x, g, b):
            m = jnp.mean(x, axis=-1, keepdims=True)
            v = jnp.mean(jnp.square(x - m), axis=-1, keepdims=True)
            return (x - m) * jax.lax.rsqrt(v + EPS) * g + b
        q = (x @ Wq + bq).reshape(N, H, HEAD)
        k = (x @ Wk + bk).reshape(N, H, HEAD)
        v = (x @ Wv + bv).reshape(N, H, HEAD)
        scores = jnp.einsum('nhd,mhd->nhm', q, k) / np.sqrt(HEAD)
        adj = jnp.zeros((N, N), jnp.float32).at[edge_index[0], edge_index[1]].set(1.0)
        scores = jnp.where(adj[:, None, :] == 0, -1000000000.0, scores)
        attn = jax.nn.softmax(scores, axis=1)
        attn_out = jnp.einsum('nhm,mhd->nhd', attn, v).reshape(N, D_OUT)
        attn_out = attn_out @ Wo + bo
        h1 = _layer_norm(x + attn_out, g1, be1)
        ff = jax.nn.relu(h1 @ W1 + b1) @ W2 + b2
        return _layer_norm(h1 + ff, g2, be2)

    def _L3_gnn_ref(x, edge_index, W, b):
        import jax, jax.numpy as jnp
        import numpy as np
        N_NODES = 6250
        IN_CH = 512
        OUT_CH = 512
        N_EDGES = 100000
        src, dst = (edge_index[0], edge_index[1])
        src_feats = x[src]
        neighbor_sum = jax.ops.segment_sum(src_feats, dst, num_segments=x.shape[0])
        neighbor_count = jax.ops.segment_sum(jnp.ones((src.shape[0],), dtype=x.dtype), dst, num_segments=x.shape[0])
        neighbor_count = jnp.maximum(neighbor_count, 1.0)
        neighbor_mean = neighbor_sum / neighbor_count[:, None]
        h = jnp.concatenate([x, neighbor_mean], axis=-1)
        return h @ W.T + b
    edge_index = jnp.stack([src, dst])
    x = _layernorm(x + _L0_gnn_ref(x, edge_index, edge_weight, L0_gnn_Wqkv, L0_gnn_bqkv, L0_gnn_Wo, L0_gnn_bo, L0_gnn_W1, L0_gnn_b1, L0_gnn_g1, L0_gnn_beta1, L0_gnn_g2, L0_gnn_beta2), axis=-1)
    x = _layernorm(x + _L1_gnn_ref(x, L1_gnn_wc, L1_gnn_wn, L1_gnn_bias, edge_index), axis=-1)
    x = _layernorm(x + _L2_gnn_ref(x, edge_index, L2_gnn_Wq, L2_gnn_bq, L2_gnn_Wk, L2_gnn_bk, L2_gnn_Wv, L2_gnn_bv, L2_gnn_Wo, L2_gnn_bo, L2_gnn_W1, L2_gnn_b1, L2_gnn_W2, L2_gnn_b2, L2_gnn_g1, L2_gnn_be1, L2_gnn_g2, L2_gnn_be2), axis=-1)
    x = _layernorm(x + _L3_gnn_ref(x, edge_index, L3_gnn_W, L3_gnn_b), axis=-1)
    return x

_drawn_inputs = setup_inputs


def setup_inputs(seed=0):
    import zlib

    import numpy as np

    out = dict(_drawn_inputs(seed))
    spreads = {'L0_gnn_bqkv': (0.0, 0.1),
     'L0_gnn_bo': (0.0, 0.1),
     'L0_gnn_b1': (0.0, 0.1),
     'L0_gnn_g1': (1.0, 0.2),
     'L0_gnn_beta1': (0.0, 0.1),
     'L0_gnn_g2': (1.0, 0.2),
     'L0_gnn_beta2': (0.0, 0.1),
     'L2_gnn_bq': (0.0, 0.8),
     'L2_gnn_bk': (0.0, 0.8),
     'L2_gnn_bv': (0.0, 0.1),
     'L2_gnn_bo': (0.0, 0.8),
     'L2_gnn_b1': (0.0, 0.1),
     'L2_gnn_b2': (0.0, 0.1),
     'L2_gnn_g1': (1.0, 0.2),
     'L2_gnn_be1': (0.0, 0.1),
     'L2_gnn_g2': (1.0, 0.2),
     'L2_gnn_be2': (0.0, 0.1)}
    factors = {'L3_gnn_b': 3.791}
    for name, (base, spread) in spreads.items():
        noise = np.random.default_rng([zlib.crc32(name.encode()), seed]).standard_normal(out[name].shape)
        drawn = base * np.exp(spread * noise) if base else spread * noise
        out[name] = jnp.asarray(drawn.astype(out[name].dtype))
    for name, factor in factors.items():
        out[name] = (out[name] * factor).astype(out[name].dtype)
    return out
```

```python
import concourse.bass as bass
from concourse import mybir
from contextlib import ExitStack

FP32 = mybir.dt.float32
BF16 = mybir.dt.bfloat16
FP16 = mybir.dt.float16
I32 = mybir.dt.int32
ALU = mybir.AluOpType
ACT = mybir.ActivationFunctionType
AX = mybir.AxisListType

P = 128
N = 512
D = 512
NB = N // P
H = 8
HD = D // H
E_ = 16384
NT = E_ // P
NG = NT // 2
WIN = 32
NWIN = N // WIN
GI = 4
NI = NG // GI
NEG = -1000000000.0
EPS = 1e-05
SCALE = HD ** -0.5
R = 4



def ring_order():
    order = []

    def add(stage, index, engine):
        order.append(((stage,) + tuple(index), engine))

    for b in range(NB):
        add("QT", (b,), "A")
    for b in range(NB):
        add("KT", (b,), "A")
    for b in range(NB):
        add("V", (b,), "D")
    for b in range(NB):
        add("BD", (b,), "D")
    for b in range(NB):
        add("AD", (b,), "A")
    for b in range(NB):
        add("S", (0, b), "D")
    for h in range(H):
        for b in range(NB):
            if h + 1 < H:
                add("S", (h + 1, b), "D")
            add("PT", (h, b), "AD"[b % 2])
    for b in range(NB):
        add("OT", (b,), "A")
    for b in range(NB):
        add("WO", (b,), "D")
    for b in range(NB + 1):
        if b < NB:
            add("HT", (b,), "A")
        if b:
            add("W1", (b - 1,), "D")
    for b in range(NB + 1):
        if b < NB:
            add("X1T", (b,), "A")
        if b:
            add("BETA", (b - 1,), "A")
            add("ALPHA", (b - 1,), "D")
    for b in range(NB):
        add("SUM", (b,), "D")
    for b in range(NB):
        add("X2T", (b,), "A")
    for b in range(NB):
        add("KT2", (b,), "A")
    for b in range(NB):
        add("QT2", (b,), "A")
    for b in range(NB):
        add("V2", (b,), "D")
    for m in range(NB):
        for h in range(H):
            add("ST", (m, h), "A")
    for b in range(NB):
        add("OT2", (b,), "A")
    for b in range(NB):
        add("WO2", (b,), "D")
    for b in range(NB):
        add("HT2", (b,), "A")
    for f in range(2 * NB):
        add("FT", (f,), "A")
    for b in range(NB):
        add("FF", (b,), "D")
    for b in range(NB + 1):
        if b < NB:
            add("X3T", (b,), "A")
        if b:
            add("Z1", (b - 1,), "D")
    for b in range(NB):
        add("NST", (b,), "A")
    for b in range(NB):
        add("Z2", (b,), "D")
    return order


ORDER = ring_order()
POS = {name: k for k, (name, _) in enumerate(ORDER)}
EMPTIED = {}
for _k, (_name, _engine) in enumerate(ORDER):
    EMPTIED[_name] = (_engine, 1 + sum(e == _engine for _, e in ORDER[:_k]))

VECTORS_0 = ["bv0", "bo0", "b10", "g10", "be10", "g20", "be20"]
VECTORS_2 = ["bv2", "bo2", "b22", "g12", "be12", "g22", "be22"]


def gnn_program(nc, a, out):
    ctx = ExitStack()
    with ctx:
        def sb(name, shape, dt=FP32):
            return ctx.enter_context(nc.sbuf_tensor(name, shape, dt))

        def sem(name):
            return ctx.enter_context(nc.semaphore(name))

        key_dram = nc.dram_tensor("key_scratch", [NT, P], FP32, kind="Internal").ap()

        X = sb("X", [P, NB, D])
        XT = sb("XT", [P, NB, N])
        HH = sb("HH", [P, NB, D])
        RB = sb("RB", [P, NB, D])
        QB = sb("QB", [P, NB, N])
        KB = sb("KB", [P, NB, N])
        VB = sb("VB", [P, NB, D])
        WA = sb("WA", [P, 3, NB, D])
        WB = sb("WB", [P, NB, D])
        WC = sb("WC", [P, NB, D])
        A_SD = sb("A_SD", [P, NB, N])
        W_SD = sb("W_SD", [P, NB, N])
        G = sb("G", [P, E_])
        probs = G[:, 0:8 * N].rearrange("p (b n) -> p b n", b=8)
        probsT = G[:, 4096:8192].rearrange("p (s m n) -> p s m n", s=2, m=NB)
        wcn = G[:, 8192:12288].rearrange("p (w k n) -> p w k n", w=2, k=NB)
        A_DS = G[:, 12288:14336].rearrange("p (k n) -> p k n", k=NB)
        B_DS = G[:, 14336:16384].rearrange("p (k n) -> p k n", k=NB)
        sT = G[:, 0:8192].rearrange("p (s h n) -> p s h n", s=2, h=H)
        max_tree = G[:, 8192:10240].rearrange("p (h n) -> p h n", h=4)
        sum_tree = G[:, 10240:12288].rearrange("p (h n) -> p h n", h=4)
        FT = G[:, 0:4096].rearrange("p (f n) -> p f n", f=2 * NB)
        vec = sb("vec", [P, 9, D])
        col = sb("col", [P, 6, NB])
        q0s = sb("q0s", [P, 2, NB])
        ident = sb("ident", [P, P])
        ones_row = sb("ones_row", [1, P])
        eps = sb("eps", [P, 1])
        st = sb("st", [P, 2, 8])
        mv = sb("mv", [P, 2, 2])
        sd = sb("sd", [P, 2, 1])
        rstd = sb("rstd", [P, 2, 1])
        nmax = sb("nmax", [P, H * NB])
        psum_of = sb("psum_of", [P, H * NB])
        rsum = sb("rsum", [P, H * NB])
        cnt_s = sb("cnt_s", [P, NB])
        cnt_d = sb("cnt_d", [P, NB])
        rc = sb("rc", [P, 2, NB])
        base_row = sb("base_row", [1, NG + 8])
        base_i = sb("base_i", [1, NG], I32)
        window_i = sb("window_i", [1, NWIN], I32)
        wide_i = sb("wide_i", [1, 1], I32)
        row = sb("row", [1, 4 * P])
        hf = HH[:, :, :].rearrange("p b n -> p (b n)")
        src_i = hf[:, 0:128].bitcast(I32)
        dst_i = hf[:, 128:256].bitcast(I32)
        nat = hf[:, 256:768].rearrange("p (k e) -> p k e", k=4)
        tr = sb("tr", [P, 4, NT + 2])
        srcT, dstT, ewT, keyT = (tr[:, k, :] for k in range(4))
        later_mask = hf[:, 768:1024]
        junk = hf[:, 1024:1280].bitcast(BF16).rearrange("p (s e) -> p s e", s=2)
        later = hf[:, 1280:1408]
        dstrel = hf[:, 1408:1536]
        w_rest = hf[:, 1536:1664]
        parts = hf[:, 1664:1856].bitcast(BF16).rearrange("p (t k) -> p t k", k=3)
        iota_w = hf[:, 1856:1872].bitcast(FP16)
        mm = hf[:, 1872:1874]
        base_bc = hf[:, 1874:1874 + NG]
        rf = RB[:, :, :].rearrange("p b n -> p (b n)")
        oh = rf[:, 0:1024].bitcast(BF16).rearrange("p (g t n) -> p g t n", g=2, t=2)
        rhs = rf[:, 1024:2048].bitcast(BF16).rearrange("p (s t k n) -> p s t k n", s=2, t=2 * GI, k=4)
        iota_n = sb("iota_n", [P, N], FP16)
        cnt_g = sb("cnt_g", [P, 2, NB, WIN])

        bank = [ctx.enter_context(nc.psum_tensor(f"bank{i}", [P, 512], FP32)) for i in range(8)]
        ring = bank[4:8]
        group_bank = [bank[i][:, 0:NB * 2 * WIN].rearrange("p (b k n) -> p b k n", b=NB, k=2) for i in range(2)]

        loads = {}

        def load_sem(name):
            loads[name] = sem("ld_" + name)
            return loads[name]

        ring_full = sem("ring_full")
        act_emptied = sem("act_emptied")
        dve_emptied = sem("dve_emptied")
        key_ready = sem("key_ready")
        key_stored = sem("key_stored")
        edges_float = sem("edges_float")
        tile_ranges = sem("tile_ranges")
        edges_turned = sem("edges_turned")
        ranges_turned = sem("ranges_turned")
        base_ready = sem("base_ready")
        base_spread = sem("base_spread")
        consts = sem("consts")
        zeroed = sem("zeroed")
        diag_set = sem("diag_set")
        compared = sem("compared")
        flags_done = sem("flags_done")
        rhs_ready = sem("rhs_ready")
        rhs_part = sem("rhs_part")
        onehot_ready = sem("onehot_ready")
        group_full = sem("group_full")
        count_ready = sem("count_ready")
        bias_cleared = sem("bias_cleared")
        group_folded = sem("group_folded")
        group_added = sem("group_added")
        bias_built = sem("bias_built")
        count_built = sem("count_built")
        dve_step = sem("dve_step")
        act_step = sem("act_step")
        pool_step = sem("pool_step")
        exp_done = sem("exp_done")
        out_full = sem("out_full")
        head_done = sem("head_done")
        out_taken = sem("out_taken")
        stats_ready = sem("stats_ready")
        std_ready = sem("std_ready")
        h_ready = sem("h_ready")
        x_ready = sem("x_ready")
        resid_ready = sem("resid_ready")
        degree_ready = sem("degree_ready")
        centered = sem("centered")
        soft_exp = sem("soft_exp")
        soft_sum = sem("soft_sum")
        soft_ready = sem("soft_ready")
        notadj_ready = sem("notadj_ready")
        out_stored = sem("out_stored")

        NADJ = sb("NADJ", [P, N])

        block = ctx.enter_context(nc.Block())

        def wait_emptied(eng, name):
            engine, count = EMPTIED[name]
            eng.wait_ge(act_emptied if engine == "A" else dve_emptied, count)

        def wait_full(eng, name):
            eng.wait_ge(ring_full, POS[name] + 1)

        def bank_of(name):
            return ring[POS[name] % R]

        def blocks(w):
            return w.rearrange("(k p) n -> p k n", p=P)

        all_loads = ["src", "dst", "ew", "xT", "wq0", "wk0", "wv0", "x", "wo0", "w10", "wcn", "bias1", "b3",
                     "col", "wqkv2", "wo2", "w12a", "w12b", "w22", "w3a", "w3b"] + VECTORS_0 + VECTORS_2 + \
                    [f"key{c}" for c in range(4)]
        for name in all_loads:
            load_sem(name)
        slot = {v: i for i, v in enumerate(VECTORS_0)} | {v: i for i, v in enumerate(VECTORS_2)} | \
            {"bias1": 7, "b3": 8}

        @block.sync
        def _(sp):
            def load(name, dst, src):
                sp.dma_start(dst, src).then_inc(loads[name], 16)

            def load_vector(name):
                load(name, vec[:, slot[name], :], a[name].partition_broadcast(P))

            load("dst", dst_i, a["dst"].rearrange("(t e) -> t e", e=P))
            load("src", src_i, a["src"].rearrange("(t e) -> t e", e=P))
            load("ew", nat[:, 2, :], a["ew"].rearrange("(t e) -> t e", e=P))
            load("xT", XT[:, :, :], blocks(a["xT"]))
            load("wq0", WA[:, 0, :, :], blocks(a["wqkv0"][:, 0:D]))
            load("col", col[:, :, :], a["cols"].rearrange("p (g k) -> p g k", k=NB))
            sp.wait_ge(key_ready, 1)
            sp.dma_start(key_dram, nat[:, 3, :]).then_inc(key_stored, 16)
            load("wk0", WA[:, 1, :, :], blocks(a["wqkv0"][:, D:2 * D]))
            sp.wait_ge(key_stored, 16)
            flat = key_dram.rearrange("t e -> (t e)")
            for c in range(4):
                load(f"key{c}", G[:, c * 4096:(c + 1) * 4096], flat[c * 4096:(c + 1) * 4096].partition_broadcast(P))
                if c == 0:
                    load("wv0", WA[:, 2, :, :], blocks(a["wqkv0"][:, 2 * D:3 * D]))
                    load("bv0", vec[:, slot["bv0"], :], a["bqkv0"][2 * D:3 * D].partition_broadcast(P))
            load("x", X[:, :, :], blocks(a["x"]))
            load("wo0", WB[:, :, :], blocks(a["wo0"]))
            load("w10", WC[:, :, :], blocks(a["w10"]))
            for v in VECTORS_0[1:] + ["bias1", "b3"]:
                load_vector(v)
            sp.wait_ge(flags_done, 1)
            sp.dma_start(wcn[:, 0, :, :], blocks(a["wc"])).then_inc(loads["wcn"], 16)
            sp.dma_start(wcn[:, 1, :, :], blocks(a["wn"])).then_inc(loads["wcn"], 16)
            wait_full(sp, ("V", NB - 1))
            for k, w in enumerate(("wq2", "wk2", "wv2")):
                sp.dma_start(WA[:, k, :, :], blocks(a[w])).then_inc(loads["wqkv2"], 16)
            wait_full(sp, ("BD", NB - 1))
            load("w12b", W_SD[:, :, :], blocks(a["w12"][:, D:2 * D]))
            wait_full(sp, ("WO", NB - 1))
            load("wo2", WB[:, :, :], blocks(a["wo2"]))
            wait_full(sp, ("W1", NB - 1))
            load("w12a", WC[:, :, :], blocks(a["w12"][:, 0:D]))
            sp.wait_ge(x_ready, NB)
            for v in VECTORS_2:
                load_vector(v)
            wait_full(sp, ("V2", NB - 1))
            load("w22", WA[:, 0:2, :, :], a["w22"].rearrange("(g k p) n -> p g k n", p=P, k=NB))
            load("w3a", WA[:, 2, :, :], blocks(a["w3"][0:D, :]))
            wait_full(sp, ("WO2", NB - 1))
            load("w3b", WB[:, :, :], blocks(a["w3"][D:2 * D, :]))
            for b in range(NB):
                sp.wait_ge(h_ready, 2 * NB + b + 1)
                sp.dma_start(out[b * P:(b + 1) * P, :], HH[:, b, :]).then_inc(out_stored, 16)
            sp.wait_ge(out_stored, 16 * NB)

        @block.gpsimd
        def _(pool):
            steps = [0]

            def link(ins):
                steps[0] += 1
                ins.then_inc(pool_step, 1)
                pool.wait_ge(pool_step, steps[0])

            link(pool.memset(ident[:, :], 0.0))
            pool.affine_select(out=ident[:, :], in_=ident[:, :], compare_op=ALU.not_equal, fill=1.0, base=0,
                               pattern=[[-1, P]], channel_multiplier=1).then_inc(consts, 1)
            pool.memset(ones_row[:, :], 1.0).then_inc(consts, 1)
            pool.memset(eps[:, :], EPS).then_inc(consts, 1)
            pool.iota(iota_n[:, :], pattern=[[1, N]], base=0, channel_multiplier=0,
                      allow_small_or_imprecise_dtypes=True).then_inc(consts, 1)
            pool.iota(iota_w, pattern=[[1, WIN]], base=0, channel_multiplier=0,
                      allow_small_or_imprecise_dtypes=True).then_inc(consts, 1)
            link(pool.memset(later_mask, 1.0))
            pool.affine_select(out=later_mask, in_=later_mask, compare_op=ALU.is_gt, fill=0.0, base=0,
                               pattern=[[1, 2 * P]], channel_multiplier=-1).then_inc(consts, 1)
            pool.memset(A_SD[:, :, :], 0.0).then_inc(zeroed, 1)
            link(pool.memset(W_SD[:, :, :], NEG))
            for b in range(NB):
                pool.affine_select(out=W_SD[:, b, :], in_=W_SD[:, b, :], compare_op=ALU.not_equal, fill=0.0,
                                   base=b * P, pattern=[[-1, N]], channel_multiplier=1).then_inc(diag_set, 1)
            pool.iota(window_i[:, :], pattern=[[WIN, NWIN]], base=0, channel_multiplier=0).then_inc(zeroed, 1)
            pool.memset(tr[:, :, NT:NT + 2], 0.0).then_inc(zeroed, 1)

            def add_counts(g, q, base):
                pool.wait_ge(count_ready, g + 1)
                pool.wait_ge(group_added, g + 2)
                win = A_SD[:, :, bass.ds(base, WIN)]
                pool.tensor_tensor(win, win, cnt_g[:, q % 2, :, :], ALU.add).then_inc(group_added, 1)

            pool.wait_ge(base_ready, 1)
            pool.wait_ge(zeroed, 3)
            pool.engine_nop().then_inc(group_added, 2)
            wide = pool.value_load(wide_i[0:1, 0:1], min_val=0, max_val=1)
            with pool.If(wide < 1):
                with pool.Fori(0, NI) as i:
                    for q in range(GI):
                        base = pool.value_load(base_i[0:1, bass.ds(i * GI + q, 1)], min_val=0, max_val=N - WIN)
                        add_counts(i * GI + q, q, base)
            with pool.Else():
                with pool.Fori(0, NWIN) as w:
                    with pool.Fori(0, NI) as i:
                        for q in range(GI):
                            base = pool.value_load(window_i[0:1, bass.ds(w, 1)], min_val=0, max_val=N - WIN)
                            add_counts(w * NG + i * GI + q, q, base)
            pool.engine_nop().then_inc(count_built, 1)

            def resid(out_, x_, vector):
                pool.tensor_tensor(out_, x_, vec[:, slot[vector], :], ALU.add).then_inc(resid_ready, 1)

            pool.wait_ge(bias_built, 1)
            pool.wait_ge(loads["x"], 16)
            pool.wait_ge(loads["bo0"], 16)
            pool.wait_ge(loads["be20"], 16)
            for b in range(NB):
                resid(RB[:, b, :], X[:, b, :], "bo0")
            for b in range(NB):
                if b == 0:
                    pool.wait_ge(head_done, H)
                resid(QB[:, b, :], X[:, b, :], "be20")
            pool.wait_ge(loads["b10"], 16)
            for b in range(NB):
                pool.wait_ge(h_ready, b + 1)
                resid(RB[:, b, :], HH[:, b, :], "b10")
            pool.wait_ge(loads["bias1"], 16)
            for b in range(NB):
                pool.wait_ge(x_ready, b + 1)
                resid(RB[:, b, :], X[:, b, :], "bias1")
            pool.wait_ge(loads["bo2"], 16)
            for b in range(NB):
                pool.wait_ge(x_ready, NB + b + 1)
                resid(RB[:, b, :], X[:, b, :], "bo2")
            for m in range(NB):
                pool.wait_ge(soft_exp, m + 1)
                if m:
                    pool.wait_ge(soft_ready, m)
                s = sT[:, m % 2, :, :]
                link(pool.tensor_tensor(sum_tree[:, :, :], s[:, 0:4, :], s[:, 4:8, :], ALU.add))
                link(pool.tensor_tensor(sum_tree[:, 0:2, :], sum_tree[:, 0:2, :], sum_tree[:, 2:4, :], ALU.add))
                pool.tensor_tensor(sum_tree[:, 0, :], sum_tree[:, 0, :], sum_tree[:, 1, :],
                                   ALU.add).then_inc(soft_sum, 1)
            pool.wait_ge(loads["be22"], 16)
            pool.wait_ge(out_full, 2 * NB)
            for b in range(NB):
                resid(VB[:, b, :], X[:, b, :], "be22")
            pool.wait_ge(loads["b22"], 16)
            for b in range(NB):
                pool.wait_ge(h_ready, NB + b + 1)
                resid(RB[:, b, :], HH[:, b, :], "b22")
            for b in range(NB):
                pool.wait_ge(x_ready, 2 * NB + b + 1)
                resid(RB[:, b, :], X[:, b, :], "b3")

        @block.scalar
        def _(act):
            act.wait_ge(loads["col"], 16)
            act.activation(q0s[:, 0, :], col[:, 0, :], ACT.Copy, scale=SCALE).then_inc(act_step, 1)
            act.activation(q0s[:, 1, :], col[:, 2, :], ACT.Copy, scale=SCALE).then_inc(act_step, 1)
            act.wait_ge(act_step, 2)

            def evac(name, dst, bias=None, scale=1.0, func=ACT.Identity, src=None):
                wait_full(act, name)
                src = bank_of(name)[:, :] if src is None else src(bank_of(name))
                if bias is None:
                    ins = act.activation(dst, src, ACT.Copy, scale=scale)
                else:
                    ins = act.activation(dst, src, func, bias=bias, scale=scale)
                ins.then_inc(act_emptied, 1)

            def turned(name, dst, b):
                evac(name, dst[:, :, b * P:(b + 1) * P], src=lambda t: t[:, :].rearrange("p (k n) -> p k n", k=NB))

            n_std = [0]

            def std():
                act.wait_ge(stats_ready, n_std[0] + 1)
                k = n_std[0] % 2
                act.activation(sd[:, k, :], mv[:, k, 1:2], ACT.Sqrt, bias=eps[:, :]).then_inc(std_ready, 1)
                n_std[0] += 1

            for b in range(NB):
                evac(("QT", b), QB[:, b, :], bias=q0s[:, 0, b:b + 1], scale=SCALE)
            for b in range(NB):
                evac(("KT", b), KB[:, b, :], bias=col[:, 1, b:b + 1])

            def take_counts(g, q):
                act.wait_ge(group_full, g + 1)
                act.wait_ge(group_added, g + 1)
                act.activation(cnt_g[:, q % 2, :, :], group_bank[q % 2][:, :, 0, :], ACT.Copy).then_inc(count_ready, 1)

            act.wait_ge(base_ready, 1)
            wide = act.value_load(wide_i[0:1, 0:1], min_val=0, max_val=1)
            with act.If(wide < 1):
                with act.Fori(0, NI) as i:
                    for q in range(GI):
                        take_counts(i * GI + q, q)
            with act.Else():
                with act.Fori(0, NWIN) as w:
                    with act.Fori(0, NI) as i:
                        for q in range(GI):
                            take_counts(w * NG + i * GI + q, q)

            for b in range(NB):
                evac(("AD", b), A_DS[:, b, :])
            def exp0(h, b):
                k = h * NB + b
                act.wait_ge(dve_emptied, EMPTIED[("S", h, b)][1])
                act.activation(probs[:, k % 8, :], probs[:, k % 8, :], ACT.Exp, bias=nmax[:, k:k + 1], scale=-1.0,
                               accum_out=psum_of[:, k:k + 1]).then_inc(exp_done, 1)

            for b in range(NB):
                exp0(0, b)
            for h in range(H):
                for b in range(NB):
                    if h + 1 < H:
                        exp0(h + 1, b)
                    if b % 2 == 0:
                        if b == 0 and h >= 2:
                            act.wait_ge(head_done, h - 1)
                        turned(("PT", h, b), probsT[:, h % 2, :, :], b)
            for b in range(NB):
                turned(("OT", b), XT, b)
            for b in range(NB):
                std()
                turned(("HT", b), XT, b)
            for b in range(NB + 1):
                if b < NB:
                    std()
                    std()
                    turned(("X1T", b), XT, b)
                if b:
                    evac(("BETA", b - 1), KB[:, b - 1, :])
            for b in range(NB):
                std()
            for b in range(NB):
                turned(("X2T", b), XT, b)
            for b in range(NB):
                evac(("KT2", b), KB[:, b, :], bias=col[:, 3, b:b + 1])
            for b in range(NB):
                evac(("QT2", b), QB[:, b, :], bias=q0s[:, 1, b:b + 1], scale=SCALE)

            def exp2(m):
                s = sT[:, m % 2, :, :]
                act.wait_ge(centered, m + 1)
                act.activation(s, s, ACT.Exp).then_inc(soft_exp, 1)

            for m in range(NB):
                for h in range(H):
                    if m >= 2 and h == 0:
                        act.wait_ge(head_done, H + m - 1)
                    evac(("ST", m, h), sT[:, m % 2, h, :])
                if m:
                    exp2(m - 1)
            exp2(NB - 1)
            for b in range(NB):
                act.wait_ge(out_full, NB + b + 1)
                act.activation(HH[:, b, :], bank[b][:, :], ACT.Copy).then_inc(out_taken, 1)
            for b in range(NB):
                turned(("OT2", b), XT, b)
            for b in range(NB):
                std()
                turned(("HT2", b), XT, b)
            for f in range(2 * NB):
                evac(("FT", f), FT[:, f, :], bias=col[:, 4 + f // NB, f % NB:f % NB + 1], func=ACT.Relu)
            for b in range(NB):
                std()
                std()
                turned(("X3T", b), XT, b)
            for b in range(NB):
                evac(("NST", b), QB[:, b, :])
            for b in range(NB):
                std()

        @block.vector
        def _(dve):
            steps = [0]

            def link(ins):
                steps[0] += 1
                ins.then_inc(dve_step, 1)
                dve.wait_ge(dve_step, steps[0])

            dve.wait_ge(loads["dst"], 16)
            dve.tensor_copy(nat[:, 1, :], dst_i).then_inc(edges_float, 1)
            dve.wait_ge(loads["src"], 16)
            dve.tensor_copy(nat[:, 0, :], src_i).then_inc(edges_float, 1)
            dve.wait_ge(edges_float, 2)
            dve.scalar_tensor_tensor(out=nat[:, 3, :], in0=nat[:, 1, :], scalar=float(N), in1=nat[:, 0, :],
                                     op0=ALU.mult, op1=ALU.add).then_inc(key_ready, 1)
            dve.tensor_reduce(mm[:, 0:1], nat[:, 1, :], AX.X, ALU.min).then_inc(tile_ranges, 1)
            dve.tensor_reduce(mm[:, 1:2], nat[:, 1, :], AX.X, ALU.max).then_inc(tile_ranges, 1)
            dve.wait_ge(ranges_turned, 1)
            link(dve.tensor_copy(row[:, 0:2 * P], bank[3][0:1, 0:2 * P]))
            link(dve.tensor_tensor(row[:, 2 * P:2 * P + NG], row[:, 0:P:2], row[:, 1:P:2], ALU.min))
            link(dve.tensor_tensor(row[:, 3 * P:3 * P + NG], row[:, P:2 * P:2], row[:, P + 1:2 * P:2], ALU.max))
            link(dve.tensor_scalar(base_row[:, 0:NG], row[:, 2 * P:2 * P + NG], float(N - WIN), None, ALU.min))
            link(dve.tensor_copy(base_i[:, :], base_row[:, 0:NG]))
            link(dve.tensor_tensor(row[:, 3 * P:3 * P + NG], row[:, 3 * P:3 * P + NG], base_row[:, 0:NG],
                                   ALU.subtract))
            link(dve.tensor_reduce(base_row[:, NG:NG + 1], row[:, 3 * P:3 * P + NG], AX.X, ALU.max))
            dve.tensor_scalar(wide_i[:, :], base_row[:, NG:NG + 1], float(WIN - 1), None,
                              ALU.is_gt).then_inc(base_ready, 1)
            dve.wait_ge(edges_turned, 1)
            link(dve.tensor_copy(tr[:, :, 0:NT], bank[2][:, :].rearrange("p (k t) -> p k t", k=4)))
            link(dve.tensor_copy(parts[:, :, 0], ewT[:, 0:NT]))
            link(dve.tensor_tensor(w_rest, ewT[:, 0:NT], parts[:, :, 0], ALU.subtract))
            link(dve.tensor_copy(parts[:, :, 1], w_rest))
            link(dve.tensor_tensor(w_rest, w_rest, parts[:, :, 1], ALU.subtract))
            link(dve.tensor_copy(parts[:, :, 2], w_rest))
            dve.wait_ge(base_spread, 1)
            link(dve.tensor_copy(base_bc, bank[3][:, 2 * P:2 * P + NG]))
            dve.wait_ge(consts, 6)

            dve.engine_nop().then_inc(compared, 2)
            for c in range(4):
                dve.wait_ge(loads[f"key{c}"], 16)
                with dve.Fori(0, NI // 4) as i:
                    for q in range(GI):
                        t = i * (2 * GI) + (c * (NT // 4) + 2 * q)
                        for j, width in ((0, 2 * P), (1, P)):
                            dve.wait_ge(compared, t + (j + 1))
                            dve.scalar_tensor_tensor(
                                out=junk[:, j, 0:width], in0=G[:, bass.ds(t * P + j * P, width)],
                                scalar=keyT[:, bass.ds(t + j, 1)], in1=later_mask[:, 0:width],
                                op0=ALU.is_equal, op1=ALU.mult, accum_out=later[:, bass.ds(t + j, 1)]).then_inc(compared, 1)
            dve.wait_ge(compared, NT + 2)
            link(dve.tensor_scalar(later, later, 0.0, None, ALU.is_equal))
            dve.tensor_tensor(parts, parts, later.rearrange("p (t k) -> p t k", k=1).broadcast_to([P, NT, 3]),
                              ALU.mult).then_inc(flags_done, 1)
            dve.wait_ge(flags_done, 1)
            dve.wait_ge(loads["bv0"], 16)
            for b in range(NB):
                wait_full(dve, ("V", b))
                dve.tensor_tensor(VB[:, b, :], bank_of(("V", b))[:, :], vec[:, slot["bv0"], :],
                                  ALU.add).then_inc(dve_emptied, 1)
            dve.wait_ge(diag_set, NB)
            dve.wait_ge(zeroed, 3)
            dve.engine_nop().then_inc(group_folded, 2)

            def build_rhs(turn, slot_, i):
                t0 = i * 2 * GI
                if turn is not None:
                    dve.wait_ge(group_folded, turn * GI + 2)
                eq = rhs[:, slot_, :, 0, :]
                rel = dstrel[:, bass.ds(t0, 2 * GI)].rearrange("p (t k) -> p t k", k=1)
                dve.tensor_tensor(eq, iota_w.rearrange("p (k n) -> p k n", k=1).broadcast_to([P, 2 * GI, WIN]),
                                  rel.broadcast_to([P, 2 * GI, WIN]), ALU.is_equal).then_inc(rhs_part, 1)
                return eq

            def scale_rhs(slot_, i):
                t0 = i * 2 * GI
                eq = rhs[:, slot_, :, 0:1, :]
                w = parts[:, bass.ds(t0, 2 * GI), :].rearrange("p t (k n) -> p t k n", n=1)
                dve.tensor_tensor(rhs[:, slot_, :, 1:4, :], eq.broadcast_to([P, 2 * GI, 3, WIN]),
                                  w.broadcast_to([P, 2 * GI, 3, WIN]), ALU.mult).then_inc(rhs_ready, 1)

            def onehots(t, pair):
                for j in range(2):
                    ins = dve.tensor_scalar(oh[:, pair, j, :], iota_n[:, :], srcT[:, bass.ds(t + j, 1)], None,
                                            ALU.is_equal)
                ins.then_inc(onehot_ready, 1)

            def sweep(g0, r0, base_of):
                onehots(0, 0)
                with dve.Fori(0, NI // 2) as ii:
                    for s in range(2):
                        i = ii * 2 + s
                        turn = r0 + i
                        build_rhs(turn, s, i)
                        dve.wait_ge(rhs_part, turn + 1)
                        scale_rhs(s, i)
                        for q in range(GI):
                            g = i * GI + q
                            base = base_of(g)
                            win = W_SD[:, :, bass.ds(base, WIN)]
                            dve.wait_ge(count_ready, g0 + g + 1)
                            dve.scalar_tensor_tensor(out=win, in0=cnt_g[:, q % 2, :, :], scalar=0.0, in1=win,
                                                     op0=ALU.is_equal, op1=ALU.mult).then_inc(bias_cleared, 1)
                            onehots(g * 2 + 2, (q + 1) % 2)
                            dve.wait_ge(bias_cleared, g0 + g + 1)
                            dve.tensor_tensor(win, win, group_bank[q % 2][:, :, 1, :],
                                              ALU.add).then_inc(group_folded, 1)
                            dve.wait_ge(group_folded, g0 + g + 3)

            wide = dve.value_load(wide_i[0:1, 0:1], min_val=0, max_val=1)
            with dve.If(wide < 1):
                dve.tensor_tensor(dstrel.rearrange("p (g j) -> p g j", j=2),
                                  dstT[:, 0:NT].rearrange("p (g j) -> p g j", j=2),
                                  base_bc.rearrange("p (g j) -> p g j", j=1).broadcast_to([P, NG, 2]),
                                  ALU.subtract).then_inc(dve_step, 1)
                dve.wait_ge(dve_step, steps[0] + 1)
                sweep(0, 0, lambda g: dve.value_load(base_i[0:1, bass.ds(g, 1)], min_val=0, max_val=N - WIN))
            with dve.Else():
                dve.tensor_copy(dstrel, dstT[:, 0:NT]).then_inc(dve_step, 1)
                dve.wait_ge(dve_step, steps[0] + 1)
                with dve.Fori(0, NWIN) as w:
                    sweep(w * NG, w * NI, lambda g: w * WIN)
                    dve.tensor_scalar(dstrel, dstrel, float(WIN), None, ALU.subtract).then_inc(dve_step, 1)
                    dve.wait_ge(dve_step, w + (steps[0] + 2))
            dve.engine_nop().then_inc(bias_built, 1)
            link_sem = sem("dve_link")
            count = [0]

            def link(ins):
                count[0] += 1
                ins.then_inc(link_sem, 1)
                dve.wait_ge(link_sem, count[0])

            for b in range(NB):
                wait_full(dve, ("BD", b))
                dve.tensor_copy(B_DS[:, b, :], bank_of(("BD", b))[:, :]).then_inc(dve_emptied, 1)
            dve.wait_ge(dve_emptied, EMPTIED[("BD", NB - 1)][1])

            def scores(h, b):
                k = h * NB + b
                if k >= 8:
                    wait_full(dve, ("PT", (k - 8) // NB, (k - 8) % NB))
                wait_full(dve, ("S", h, b))
                dve.tensor_tensor_reduce(out=probs[:, k % 8, :], in0=bank_of(("S", h, b))[:, :], in1=B_DS[:, b, :],
                                         scale=-1.0, scalar=3.0e38, op0=ALU.add, op1=ALU.min,
                                         accum_out=nmax[:, k:k + 1]).then_inc(dve_emptied, 1)

            for b in range(NB):
                scores(0, b)
            for h in range(H):
                for b in range(NB):
                    if h + 1 < H:
                        scores(h + 1, b)
                    if b % 2:
                        if b == 1 and h >= 2:
                            dve.wait_ge(head_done, h - 1)
                        wait_full(dve, ("PT", h, b))
                        dve.tensor_copy(probsT[:, h % 2, :, b * P:(b + 1) * P],
                                        bank_of(("PT", h, b))[:, :].rearrange("p (k n) -> p k n", k=NB)
                                        ).then_inc(dve_emptied, 1)
                if h == 1:
                    dve.wait_ge(count_built, 1)
                    dve.tensor_reduce(cnt_s[:, :], A_SD[:, :, :], AX.X, ALU.add).then_inc(degree_ready, 1)
                    wait_emptied(dve, ("AD", NB - 1))
                    dve.tensor_reduce(cnt_d[:, :], A_DS[:, :, :], AX.X, ALU.add).then_inc(degree_ready, 1)
                    dve.wait_ge(degree_ready, 2)
                    link(dve.reciprocal(rc[:, 0, :], cnt_s[:, :]))
                    link(dve.tensor_scalar(cnt_d[:, :], cnt_d[:, :], 1.0, None, ALU.max))
                    link(dve.reciprocal(rc[:, 1, :], cnt_d[:, :]))
            dve.wait_ge(exp_done, H * NB)
            link(dve.reciprocal(rsum[:, :], psum_of[:, :]))
            by_row = rsum[:, :].rearrange("p (h b) -> p b h", b=NB)
            for b in range(NB):
                dve.wait_ge(out_full, b + 1)
                dve.tensor_tensor(HH[:, b, :].rearrange("p (h d) -> p h d", h=H),
                                  bank[b][:, :].rearrange("p (h d) -> p h d", h=H),
                                  by_row[:, b, :].rearrange("p (h d) -> p h d", d=1).broadcast_to([P, H, HD]),
                                  ALU.mult).then_inc(out_taken, 1)

            n_ln = [0]
            resids = [0]

            def stats(z):
                k = n_ln[0] % 2
                link(dve.bn_stats(st[:, k, 0:6], z))
                dve.bn_aggr(mv[:, k, :], st[:, k, 0:6]).then_inc(stats_ready, 1)
                dve.wait_ge(std_ready, n_ln[0] + 1)
                link(dve.reciprocal(rstd[:, k, :], sd[:, k, :]))
                n_ln[0] += 1
                return mv[:, k, 0:1], rstd[:, k, :]

            def norm(dst, z, done):
                mu, r = stats(z)
                dve.tensor_scalar(dst, z, mu, r, ALU.subtract, ALU.mult).then_inc(done, 1)

            def norm_affine(dst, z, gain, shift, after):
                mu, r = stats(z)
                link(dve.scalar_tensor_tensor(out=z, in0=z, scalar=mu, in1=vec[:, slot[gain], :],
                                              op0=ALU.subtract, op1=ALU.mult))
                return dve.scalar_tensor_tensor(out=dst, in0=z, scalar=r, in1=shift, op0=ALU.mult, op1=ALU.add)

            def take(name, dst, resid):
                wait_full(dve, name)
                dve.tensor_tensor(dst, bank_of(name)[:, :], resid, ALU.add).then_inc(dve_emptied, 1)
                wait_emptied(dve, name)

            def take_scaled(name, dst, scale, resid):
                wait_full(dve, name)
                dve.scalar_tensor_tensor(out=dst, in0=bank_of(name)[:, :], scalar=scale, in1=resid, op0=ALU.mult,
                                         op1=ALU.add).then_inc(dve_emptied, 1)
                wait_emptied(dve, name)

            for v in ("g10", "be10", "g20"):
                dve.wait_ge(loads[v], 16)
            for b in range(NB):
                dve.wait_ge(resid_ready, b + 1)
                take(("WO", b), HH[:, b, :], RB[:, b, :])
                norm_affine(HH[:, b, :], HH[:, b, :], "g10", vec[:, slot["be10"], :], None).then_inc(h_ready, 1)
            for b in range(NB):
                dve.wait_ge(resid_ready, 2 * NB + b + 1)
                take(("W1", b), HH[:, b, :], RB[:, b, :])
                link(norm_affine(X[:, b, :], HH[:, b, :], "g20", QB[:, b, :], None))
                norm(X[:, b, :], X[:, b, :], x_ready)
            for b in range(NB):
                dve.wait_ge(resid_ready, 3 * NB + b + 1)
                take(("ALPHA", b), RB[:, b, :], RB[:, b, :])
            for b in range(NB):
                take_scaled(("SUM", b), HH[:, b, :], rc[:, 0, b:b + 1], RB[:, b, :])
                norm(X[:, b, :], HH[:, b, :], x_ready)
            dve.wait_ge(loads["bv2"], 16)
            for b in range(NB):
                wait_full(dve, ("V2", b))
                dve.tensor_tensor(VB[:, b, :], bank_of(("V2", b))[:, :], vec[:, slot["bv2"], :],
                                  ALU.add).then_inc(dve_emptied, 1)

            def center(m):
                s = sT[:, m % 2, :, :]
                if m:
                    dve.wait_ge(centered, m)
                wait_emptied(dve, ("ST", m, H - 1))
                link(dve.tensor_tensor(max_tree[:, :, :], s[:, 0:4, :], s[:, 4:8, :], ALU.max))
                link(dve.tensor_tensor(max_tree[:, 0:2, :], max_tree[:, 0:2, :], max_tree[:, 2:4, :], ALU.max))
                link(dve.tensor_tensor(max_tree[:, 0, :], max_tree[:, 0, :], max_tree[:, 1, :], ALU.max))
                dve.tensor_tensor(s, s, max_tree[:, 0:1, :].broadcast_to([P, H, N]),
                                  ALU.subtract).then_inc(centered, 1)

            def weigh(m):
                s = sT[:, m % 2, :, :]
                dve.wait_ge(soft_sum, m + 1)
                link(dve.reciprocal(max_tree[:, 1, :], sum_tree[:, 0, :]))
                link(dve.scalar_tensor_tensor(out=max_tree[:, 1, :], in0=A_DS[:, m, :], scalar=0.0,
                                              in1=max_tree[:, 1, :], op0=ALU.is_gt, op1=ALU.mult))
                if m:
                    dve.wait_ge(head_done, H + m)
                dve.tensor_scalar(NADJ[:, :], A_DS[:, m, :], 0.0, 1.0 / H, ALU.is_equal,
                                  ALU.mult).then_inc(notadj_ready, 1)
                dve.tensor_tensor(s, s, max_tree[:, 1:2, :].broadcast_to([P, H, N]), ALU.mult).then_inc(soft_ready, 1)
                dve.wait_ge(soft_ready, m + 1)

            for m in range(NB):
                center(m)
                if m:
                    weigh(m - 1)
            weigh(NB - 1)
            for v in ("g12", "be12", "g22"):
                dve.wait_ge(loads[v], 16)
            for b in range(NB):
                dve.wait_ge(resid_ready, 4 * NB + b + 1)
                take(("WO2", b), HH[:, b, :], RB[:, b, :])
                norm_affine(HH[:, b, :], HH[:, b, :], "g12", vec[:, slot["be12"], :], None).then_inc(h_ready, 1)
            for b in range(NB):
                dve.wait_ge(resid_ready, 6 * NB + b + 1)
                take(("FF", b), HH[:, b, :], RB[:, b, :])
                link(norm_affine(X[:, b, :], HH[:, b, :], "g22", VB[:, b, :], None))
                norm(X[:, b, :], X[:, b, :], x_ready)
            for b in range(NB):
                dve.wait_ge(resid_ready, 7 * NB + b + 1)
                take(("Z1", b), RB[:, b, :], RB[:, b, :])
            for b in range(NB):
                take_scaled(("Z2", b), HH[:, b, :], rc[:, 1, b:b + 1], RB[:, b, :])
                norm(HH[:, b, :], HH[:, b, :], h_ready)

        @block.tensor
        def _(pe):
            def claim(name):
                k = POS[name]
                if k >= R:
                    wait_emptied(pe, ORDER[k - R][0])
                return bank_of(name)

            def product(name, lhs, rhs_, n_k=NB):
                t = claim(name)
                for k in range(n_k):
                    last = nc.tensor.matmul(t[:, :], lhs(k), rhs_(k), start=(k == 0), stop=(k == n_k - 1))
                last.then_inc(ring_full, 1)

            def turn(name, block_of):
                t = claim(name)
                for k in range(NB):
                    last = nc.tensor.transpose(t[:, k * P:(k + 1) * P], block_of(k), ident[:, :])
                last.then_inc(ring_full, 1)

            def cols(t, k, b):
                return t[:, k, b * P:(b + 1) * P]

            pe.wait_ge(consts, 6)
            pe.wait_ge(tile_ranges, 2)
            for k in range(2):
                last = nc.tensor.matmul(bank[3][0:1, k * P:(k + 1) * P], mm[:, k:k + 1], ident[:, :], start=True,
                                        stop=True)
            last.then_inc(ranges_turned, 1)
            pe.wait_ge(loads["ew"], 16)
            for k in range(4):
                last = nc.tensor.transpose(bank[2][:, k * P:(k + 1) * P], nat[:, k, :], ident[:, :])
            last.then_inc(edges_turned, 1)
            pe.wait_ge(base_ready, 1)
            nc.tensor.matmul(bank[3][:, 2 * P:2 * P + NG], ones_row[:, :], base_row[:, 0:NG], start=True,
                             stop=True).then_inc(base_spread, 1)

            pe.wait_ge(loads["xT"], 16)
            pe.wait_ge(loads["wq0"], 16)
            for b in range(NB):
                product(("QT", b), lambda k: cols(WA[:, 0, :, :], k, b), lambda k: XT[:, k, :])
            pe.wait_ge(loads["wk0"], 16)
            for b in range(NB):
                product(("KT", b), lambda k: cols(WA[:, 1, :, :], k, b), lambda k: XT[:, k, :])
            pe.wait_ge(loads["wv0"], 16)
            for b in range(NB):
                product(("V", b), lambda k: cols(XT, k, b), lambda k: WA[:, 2, k, :])

            def group(g, oh_count, turn_count, q, s):
                pe.wait_ge(onehot_ready, oh_count)
                pe.wait_ge(rhs_ready, turn_count)
                pe.wait_ge(group_folded, g + 1)
                pe.wait_ge(group_added, g + 1)
                gb = group_bank[q % 2]
                for b in range(NB):
                    for j in range(2):
                        src1 = oh[:, q % 2, j, b * P:(b + 1) * P]
                        t = 2 * q + j
                        nc.tensor.matmul(gb[:, b, :, :], src1, rhs[:, s, t, 0:2, :], start=(j == 0), stop=False)
                        nc.tensor.matmul(gb[:, b, 1, :], src1, rhs[:, s, t, 2, :], start=False, stop=False)
                        last = nc.tensor.matmul(gb[:, b, 1, :], src1, rhs[:, s, t, 3, :], start=False,
                                                stop=(j == 1))
                last.then_inc(group_full, 1)

            wide = pe.value_load(wide_i[0:1, 0:1], min_val=0, max_val=1)
            with pe.If(wide < 1):
                with pe.Fori(0, NI // 2) as ii:
                    for s in range(2):
                        i = ii * 2 + s
                        for q in range(GI):
                            group(i * GI + q, i * GI + (q + 1), i + 1, q, s)
            with pe.Else():
                with pe.Fori(0, NWIN) as w:
                    with pe.Fori(0, NI // 2) as ii:
                        for s in range(2):
                            i = ii * 2 + s
                            for q in range(GI):
                                group(w * NG + i * GI + q, w * (NG + 1) + i * GI + (q + 1), w * NI + i + 1, q, s)

            pe.wait_ge(bias_built, 1)
            for b in range(NB):
                turn(("BD", b), lambda k: cols(W_SD, k, b))
            pe.wait_ge(count_built, 1)
            for b in range(NB):
                turn(("AD", b), lambda k: cols(A_SD, k, b))

            wait_emptied(pe, ("KT", NB - 1))

            def score(h, b):
                r = slice((h % 2) * HD, (h % 2 + 1) * HD)
                t = claim(("S", h, b))
                nc.tensor.matmul(t[:, :], QB[r, h // 2, b * P:(b + 1) * P], KB[r, h // 2, :], start=True,
                                 stop=True).then_inc(ring_full, 1)

            for b in range(NB):
                score(0, b)
            wait_emptied(pe, ("V", NB - 1))
            for h in range(H):
                for b in range(NB):
                    if h + 1 < H:
                        score(h + 1, b)
                    pe.wait_ge(exp_done, h * NB + b + 1)
                    turn(("PT", h, b), lambda k: cols(probs, (h * NB + b) % 8, k))
                wait_emptied(pe, ("PT", h, NB - 2))
                wait_emptied(pe, ("PT", h, NB - 1))
                for b in range(NB):
                    for m in range(NB):
                        last = nc.tensor.matmul(bank[b][:, h * HD:(h + 1) * HD],
                                                probsT[:, h % 2, m, b * P:(b + 1) * P],
                                                VB[:, m, h * HD:(h + 1) * HD], start=(m == 0), stop=(m == NB - 1))
                    if h == H - 1:
                        last.then_inc(out_full, 1)
                if h < H - 1:
                    last.then_inc(head_done, 1)
            pe.wait_ge(out_full, NB)
            pe.nop().then_inc(head_done, 1)
            for b in range(NB):
                pe.wait_ge(out_taken, b + 1)
                turn(("OT", b), lambda k: cols(HH, b, k))
            pe.wait_ge(loads["wo0"], 16)
            for b in range(NB):
                wait_emptied(pe, ("OT", b))
                product(("WO", b), lambda k: cols(XT, k, b), lambda k: WB[:, k, :])
            pe.wait_ge(loads["w10"], 16)
            for b in range(NB + 1):
                if b < NB:
                    pe.wait_ge(h_ready, b + 1)
                    turn(("HT", b), lambda k: cols(HH, b, k))
                if b:
                    wait_emptied(pe, ("HT", b - 1))
                    product(("W1", b - 1), lambda k: cols(XT, k, b - 1), lambda k: WC[:, k, :])
            pe.wait_ge(loads["wcn"], 32)
            for b in range(NB + 1):
                if b < NB:
                    pe.wait_ge(x_ready, b + 1)
                    turn(("X1T", b), lambda k: cols(X, b, k))
                if b:
                    wait_emptied(pe, ("X1T", b - 1))
                    product(("BETA", b - 1), lambda k: cols(XT, k, b - 1), lambda k: wcn[:, 1, k, :])
                    product(("ALPHA", b - 1), lambda k: cols(XT, k, b - 1), lambda k: wcn[:, 0, k, :])
            wait_emptied(pe, ("BETA", NB - 1))
            for b in range(NB):
                product(("SUM", b), lambda k: cols(A_DS, k, b), lambda k: KB[:, k, :])
            for b in range(NB):
                pe.wait_ge(x_ready, NB + b + 1)
                turn(("X2T", b), lambda k: cols(X, b, k))
            wait_emptied(pe, ("X2T", NB - 1))
            pe.wait_ge(loads["wqkv2"], 48)
            for b in range(NB):
                product(("KT2", b), lambda k: cols(WA[:, 1, :, :], k, b), lambda k: XT[:, k, :])
            for b in range(NB):
                product(("QT2", b), lambda k: cols(WA[:, 0, :, :], k, b), lambda k: XT[:, k, :])
            for b in range(NB):
                product(("V2", b), lambda k: cols(XT, k, b), lambda k: WA[:, 2, k, :])

            def heads_out(m):
                pe.wait_ge(notadj_ready, m + 1)
                pe.wait_ge(soft_ready, m + 1)
                for b in range(NB):
                    def others(start, stop):
                        return nc.tensor.matmul(bank[b][:, :], NADJ[:, b * P:(b + 1) * P], VB[:, m, :], start=start,
                                                stop=stop, skip_group_check=True)

                    if m < NB - 1:
                        others(m == 0, False)
                    for h in range(H):
                        last = nc.tensor.matmul(bank[b][:, h * HD:(h + 1) * HD], sT[:, m % 2, h, b * P:(b + 1) * P],
                                                VB[:, m, h * HD:(h + 1) * HD], start=False, stop=False,
                                                skip_group_check=True)
                    if m == NB - 1:
                        others(False, True).then_inc(out_full, 1)
                if m < NB - 1:
                    last.then_inc(head_done, 1)

            for m in range(NB):
                for h in range(H):
                    if m == 0 and h % 2 == 0:
                        wait_emptied(pe, ("KT2", NB - 1))
                        wait_emptied(pe, ("QT2", NB - 1))
                    r = slice((h % 2) * HD, (h % 2 + 1) * HD)
                    t = claim(("ST", m, h))
                    nc.tensor.matmul(t[:, :], KB[r, h // 2, m * P:(m + 1) * P], QB[r, h // 2, :], start=True,
                                     stop=True).then_inc(ring_full, 1)
                if m == 1:
                    wait_emptied(pe, ("V2", NB - 1))
                if m:
                    heads_out(m - 1)
            heads_out(NB - 1)
            for b in range(NB):
                pe.wait_ge(out_taken, NB + b + 1)
                turn(("OT2", b), lambda k: cols(HH, b, k))
            pe.wait_ge(loads["wo2"], 16)
            for b in range(NB):
                wait_emptied(pe, ("OT2", b))
                product(("WO2", b), lambda k: cols(XT, k, b), lambda k: WB[:, k, :])
            for b in range(NB):
                pe.wait_ge(h_ready, NB + b + 1)
                turn(("HT2", b), lambda k: cols(HH, b, k))
            wait_emptied(pe, ("HT2", NB - 1))
            pe.wait_ge(loads["w12a"], 16)
            pe.wait_ge(loads["w12b"], 16)
            for f in range(2 * NB):
                w1 = WC if f < NB else W_SD
                product(("FT", f), lambda k: cols(w1, k, f % NB), lambda k: XT[:, k, :])
            wait_emptied(pe, ("FT", 2 * NB - 1))
            pe.wait_ge(loads["w22"], 16)
            for b in range(NB):
                product(("FF", b), lambda k: cols(FT, k, b), lambda k: WA[:, k // NB, k % NB, :], n_k=2 * NB)
            pe.wait_ge(loads["w3a"], 16)
            for b in range(NB + 1):
                if b < NB:
                    pe.wait_ge(x_ready, 2 * NB + b + 1)
                    turn(("X3T", b), lambda k: cols(X, b, k))
                if b:
                    wait_emptied(pe, ("X3T", b - 1))
                    product(("Z1", b - 1), lambda k: cols(XT, k, b - 1), lambda k: WA[:, 2, k, :])
            for b in range(NB):
                product(("NST", b), lambda k: cols(X, k, b), lambda k: A_SD[:, k, :])
            wait_emptied(pe, ("NST", NB - 1))
            pe.wait_ge(loads["w3b"], 16)
            for b in range(NB):
                product(("Z2", b), lambda k: cols(QB, k, b), lambda k: WB[:, k, :])


def kernel(x, src, dst, edge_weight, L0_gnn_Wqkv, L0_gnn_bqkv, L0_gnn_Wo, L0_gnn_bo, L0_gnn_W1, L0_gnn_b1,
           L0_gnn_g1, L0_gnn_beta1, L0_gnn_g2, L0_gnn_beta2, L1_gnn_wc, L1_gnn_wn, L1_gnn_bias, L2_gnn_Wq,
           L2_gnn_bq, L2_gnn_Wk, L2_gnn_bk, L2_gnn_Wv, L2_gnn_bv, L2_gnn_Wo, L2_gnn_bo, L2_gnn_W1, L2_gnn_b1,
           L2_gnn_W2, L2_gnn_b2, L2_gnn_g1, L2_gnn_be1, L2_gnn_g2, L2_gnn_be2, L3_gnn_W, L3_gnn_b):
    import numpy as np
    import concourse.bacc as bacc
    from concourse.bass_utils import run_bass_kernel_spmd

    def turned(w):
        return np.ascontiguousarray(np.asarray(w).T)

    arrays = {
        "x": x, "xT": turned(x), "src": src, "dst": dst, "ew": edge_weight,
        "wqkv0": turned(L0_gnn_Wqkv), "bqkv0": L0_gnn_bqkv, "wo0": turned(L0_gnn_Wo), "bo0": L0_gnn_bo,
        "w10": turned(L0_gnn_W1), "b10": L0_gnn_b1, "g10": L0_gnn_g1, "be10": L0_gnn_beta1, "g20": L0_gnn_g2,
        "be20": L0_gnn_beta2, "wc": L1_gnn_wc, "wn": L1_gnn_wn, "bias1": L1_gnn_bias,
        "wq2": L2_gnn_Wq, "wk2": L2_gnn_Wk, "wv2": L2_gnn_Wv,
        "bv2": L2_gnn_bv, "wo2": L2_gnn_Wo, "bo2": L2_gnn_bo, "w12": L2_gnn_W1,
        "w22": L2_gnn_W2, "b22": L2_gnn_b2, "g12": L2_gnn_g1, "be12": L2_gnn_be1, "g22": L2_gnn_g2,
        "be22": L2_gnn_be2, "w3": turned(L3_gnn_W), "b3": L3_gnn_b,
    }
    per_feature = [np.asarray(v).reshape(-1, P).T for v in
                   (np.asarray(L0_gnn_bqkv)[:2 * D], L2_gnn_bq, L2_gnn_bk, L2_gnn_b1)]
    arrays["cols"] = np.concatenate(per_feature, axis=1)
    arrays = {f"in_{k}": np.ascontiguousarray(v) for k, v in arrays.items()}
    nc = bacc.Bacc("TRN2", target_bir_lowering=False, num_devices=1)
    aps = {k[3:]: nc.dram_tensor(k, v.shape, mybir.dt.from_np(v.dtype), kind="ExternalInput").ap()
           for k, v in arrays.items()}
    out = nc.dram_tensor("out_x", (N, D), FP32, kind="ExternalOutput").ap()
    gnn_program(nc, aps, out)
    r = run_bass_kernel_spmd(nc, [arrays], core_ids=[0])
    return r.results[0]["out_x"]
```

```python
import concourse.bass as bass
from concourse import mybir
from contextlib import ExitStack

FP32 = mybir.dt.float32
BF16 = mybir.dt.bfloat16
FP16 = mybir.dt.float16
I32 = mybir.dt.int32
ALU = mybir.AluOpType
ACT = mybir.ActivationFunctionType
AX = mybir.AxisListType

P = 128
N = 512
D = 512
NB = N // P
H = 8
HD = D // H
E_ = 16384
NT = E_ // P
NG = NT // 2
WIN = 32
NWIN = N // WIN
GI = 4
NI = NG // GI
NEG = -1000000000.0
EPS = 1e-05
SCALE = HD ** -0.5
R = 4
NU = 2 * NB
UN = N // 2
UNIT_HEADS = [0, 2, 4, 6, 1, 3, 5, 7]



def ring_order():
    order = []

    def add(stage, index, engine):
        order.append(((stage,) + tuple(index), engine))

    for b in range(NB):
        add("QT", (b,), "A")
    for b in range(NB):
        add("KT", (b,), "A")
    for b in range(NB):
        add("V", (b,), "A")
    for h in range(H):
        for b in range(NB):
            add("S", (h, b), "A")
    for b in range(NB):
        add("BD", (b,), "D")
    for b in range(NB):
        add("AD", (b,), "A")
    for h in range(H):
        for b in range(NB):
            add("PT", (h, b), "AD"[b % 2])
    for b in range(NB):
        add("OT", (b,), "A")
    for b in range(NB):
        add("WO", (b,), "D")
    for b in range(NB + 1):
        if b < NB:
            add("HT", (b,), "A")
        if b:
            add("W1", (b - 1,), "D")
    for b in range(NB + 1):
        if b < NB:
            add("X1T", (b,), "A")
        if b:
            add("BETA", (b - 1,), "A")
            add("ALPHA", (b - 1,), "D")
    for b in range(NB):
        add("SUM", (b,), "D")
    for b in range(NB):
        add("X2T", (b,), "A")
    for b in range(NB):
        add("KT2", (b,), "A")
    for b in range(NB):
        add("QT2", (b,), "A")
    for b in range(NB):
        add("V2", (b,), "D")
    for u in range(NU):
        for p in range(H // 2):
            add("ST", (u, p), "A")
    for b in range(NB):
        add("OT2", (b,), "A")
    for b in range(NB):
        add("WO2", (b,), "D")
    for b in range(NB):
        add("HT2", (b,), "A")
    for f in range(2 * NB):
        add("FT", (f,), "A")
    for b in range(NB):
        add("FF", (b,), "D")
    for b in range(NB + 1):
        if b < NB:
            add("X3T", (b,), "A")
        if b:
            add("Z1", (b - 1,), "D")
    for b in range(NB):
        add("NST", (b,), "A")
    for b in range(NB):
        add("Z2", (b,), "D")
    return order


ORDER = ring_order()
POS = {name: k for k, (name, _) in enumerate(ORDER)}
EMPTIED = {}
for _k, (_name, _engine) in enumerate(ORDER):
    EMPTIED[_name] = (_engine, 1 + sum(e == _engine for _, e in ORDER[:_k]))

VECTORS_0 = ["bv0", "bo0", "b10", "g10", "be10", "g20", "be20"]
VECTORS_2 = ["bv2", "bo2", "b22", "g12", "be12", "g22", "be22"]


def gnn_program(nc, a, out):
    ctx = ExitStack()
    with ctx:
        def sb(name, shape, dt=FP32):
            return ctx.enter_context(nc.sbuf_tensor(name, shape, dt))

        def sem(name):
            return ctx.enter_context(nc.semaphore(name))

        key_dram = nc.dram_tensor("key_scratch", [NT, P], FP32, kind="Internal").ap()

        X = sb("X", [P, NB, D])
        XT = sb("XT", [P, NB, N])
        HH = sb("HH", [P, NB, D])
        RB = sb("RB", [P, NB, D])
        QB = sb("QB", [P, NB, N])
        KB = sb("KB", [P, NB, N])
        VB = sb("VB", [P, NB, D])
        WA = sb("WA", [P, 3, NB, D])
        WB = sb("WB", [P, NB, D])
        WC = sb("WC", [P, NB, D])
        A_SD = sb("A_SD", [P, NB, N])
        W_SD = sb("W_SD", [P, NB, N])
        G = sb("G", [P, E_])
        probs = G[:, :].rearrange("p (k n) -> p k n", n=N)
        wqkv2 = G[:, 0:6144].rearrange("p (w k n) -> p w k n", w=3, k=NB)
        wcn = G[:, 8192:12288].rearrange("p (w k n) -> p w k n", w=2, k=NB)
        w22 = G[:, 12288:16384].rearrange("p (k n) -> p k n", k=2 * NB)
        sT = G[:, 0:8192].rearrange("p (s h n) -> p s h n", s=4, h=H)
        max_tree = G[:, 8192:9216].rearrange("p (h n) -> p h n", h=4)
        sum_tree = G[:, 9216:11264].rearrange("p (s h n) -> p s h n", s=2, h=4)
        share = G[:, 11264:11520]
        FT = G[:, 0:4096].rearrange("p (f n) -> p f n", f=2 * NB)
        A_DS = WA[:, 0, :, :]
        B_DS = WA[:, 1, :, :]
        probsT = [XT, WA[:, 2, :, :]]
        vec = sb("vec", [P, 9, D])
        col = sb("col", [P, 6, NB])
        q0s = sb("q0s", [P, 2, NB])
        ident = sb("ident", [P, P])
        ones_row = sb("ones_row", [1, P])
        eps = sb("eps", [P, 1])
        st = sb("st", [P, 2, 8])
        mv = sb("mv", [P, 2, 2])
        sd = sb("sd", [P, 2, 1])
        rstd = sb("rstd", [P, 2, 1])
        nmax = sb("nmax", [P, H * NB])
        psum_of = sb("psum_of", [P, H * NB])
        rsum = sb("rsum", [P, H * NB])
        cnt_s = sb("cnt_s", [P, NB])
        cnt_d = sb("cnt_d", [P, NB])
        rc = sb("rc", [P, 2, NB])
        base_row = sb("base_row", [1, NG + 8])
        base_i = sb("base_i", [1, NG], I32)
        window_i = sb("window_i", [1, NWIN], I32)
        wide_i = sb("wide_i", [1, 1], I32)
        row = sb("row", [1, 4 * P])
        hf = HH[:, :, :].rearrange("p b n -> p (b n)")
        src_i = hf[:, 0:128].bitcast(I32)
        dst_i = hf[:, 128:256].bitcast(I32)
        nat = hf[:, 256:768].rearrange("p (k e) -> p k e", k=4)
        tr = sb("tr", [P, 4, NT + 4])
        srcT, dstT, ewT, keyT = (tr[:, k, :] for k in range(4))
        later_mask = hf[:, 768:1024]
        later = hf[:, 1024:1152]
        w_rest = hf[:, 1152:1280]
        dstrel = hf[:, 1280:1280 + NT + 2 * GI]
        parts = hf[:, 1416:1416 + 3 * (NT + 2 * GI) // 2].bitcast(BF16).rearrange("p (t k) -> p t k", k=3)
        iota_w = hf[:, 1620:1636].bitcast(FP16)
        mm = hf[:, 1636:1638]
        base_bc = hf[:, 1638:1638 + NG]
        rf = RB[:, :, :].rearrange("p b n -> p (b n)")
        junk = rf[:, 0:1024].bitcast(BF16).rearrange("p (s e) -> p s e", s=2 * GI)
        rhs = rf[:, 1024:2048].bitcast(BF16).rearrange("p (s t k n) -> p s t k n", s=2, t=2 * GI, k=4)
        oh = X[:, :, :].rearrange("p b n -> p (b n)").bitcast(BF16).rearrange("p (g t n) -> p g t n", g=4, t=2)
        iota_n = sb("iota_n", [P, N], FP16)
        cnt_g = sb("cnt_g", [P, 2, NB, WIN])

        bank = [ctx.enter_context(nc.psum_tensor(f"bank{i}", [P, 512], FP32)) for i in range(8)]
        ring = bank[4:8]
        group_bank = [bank[i][:, 0:NB * 2 * WIN].rearrange("p (b k n) -> p b k n", b=NB, k=2) for i in range(2)]

        loads = {}

        def load_sem(name):
            loads[name] = sem("ld_" + name)
            return loads[name]

        ring_full = sem("ring_full")
        act_emptied = sem("act_emptied")
        dve_emptied = sem("dve_emptied")
        key_ready = sem("key_ready")
        key_stored = sem("key_stored")
        edges_float = sem("edges_float")
        tile_ranges = sem("tile_ranges")
        edges_turned = sem("edges_turned")
        ranges_turned = sem("ranges_turned")
        base_ready = sem("base_ready")
        base_spread = sem("base_spread")
        consts = sem("consts")
        zeroed = sem("zeroed")
        diag_set = sem("diag_set")
        compared = sem("compared")
        flags_done = sem("flags_done")
        rhs_ready = sem("rhs_ready")
        rhs_part = sem("rhs_part")
        onehot_ready = sem("onehot_ready")
        group_full = sem("group_full")
        count_ready = sem("count_ready")
        bias_cleared = sem("bias_cleared")
        group_folded = sem("group_folded")
        group_added = sem("group_added")
        bias_built = sem("bias_built")
        count_built = sem("count_built")
        dve_step = sem("dve_step")
        act_step = sem("act_step")
        pool_step = sem("pool_step")
        row_max = sem("row_max")
        exp_done = sem("exp_done")
        out_full = sem("out_full")
        head_done = sem("head_done")
        out_taken = sem("out_taken")
        stats_ready = sem("stats_ready")
        std_ready = sem("std_ready")
        h_ready = sem("h_ready")
        x_ready = sem("x_ready")
        resid_ready = sem("resid_ready")
        degree_ready = sem("degree_ready")
        centered = sem("centered")
        soft_exp = sem("soft_exp")
        soft_sum = sem("soft_sum")
        soft_ready = sem("soft_ready")
        notadj_ready = sem("notadj_ready")
        out_stored = sem("out_stored")

        NADJ = sb("NADJ", [P, 2, UN])

        block = ctx.enter_context(nc.Block())

        def wait_emptied(eng, name):
            engine, count = EMPTIED[name]
            eng.wait_ge(act_emptied if engine == "A" else dve_emptied, count)

        def wait_full(eng, name):
            eng.wait_ge(ring_full, POS[name] + 1)

        def bank_of(name):
            return ring[POS[name] % R]

        def blocks(w):
            return w.rearrange("(k p) n -> p k n", p=P)

        all_loads = ["src", "dst", "ew", "xT", "wq0", "wk0", "wv0", "x", "wo0", "w10", "wcn", "bias1", "b3",
                     "col", "wqkv2", "wo2", "w12a", "w12b", "w22", "w3a", "w3b"] + VECTORS_0 + VECTORS_2 + \
                    [f"key{c}" for c in range(4)]
        for name in all_loads:
            load_sem(name)
        slot = {v: i for i, v in enumerate(VECTORS_0)} | {v: i for i, v in enumerate(VECTORS_2)} | \
            {"bias1": 7, "b3": 8}

        @block.sync
        def _(sp):
            def load(name, dst, src):
                sp.dma_start(dst, src).then_inc(loads[name], 16)

            def load_vector(name):
                load(name, vec[:, slot[name], :], a[name].partition_broadcast(P))

            load("dst", dst_i, a["dst"].rearrange("(t e) -> t e", e=P))
            load("src", src_i, a["src"].rearrange("(t e) -> t e", e=P))
            load("ew", nat[:, 2, :], a["ew"].rearrange("(t e) -> t e", e=P))
            load("xT", XT[:, :, :], blocks(a["xT"]))
            load("wq0", WA[:, 0, :, :], blocks(a["wqkv0"][:, 0:D]))
            load("col", col[:, :, :], a["cols"].rearrange("p (g k) -> p g k", k=NB))
            sp.wait_ge(key_ready, 1)
            sp.dma_start(key_dram, nat[:, 3, :]).then_inc(key_stored, 16)
            load("wk0", WA[:, 1, :, :], blocks(a["wqkv0"][:, D:2 * D]))
            sp.wait_ge(key_stored, 16)
            flat = key_dram.rearrange("t e -> (t e)")
            for c in range(4):
                load(f"key{c}", G[:, c * 4096:(c + 1) * 4096], flat[c * 4096:(c + 1) * 4096].partition_broadcast(P))
                if c == 0:
                    load("wv0", WA[:, 2, :, :], blocks(a["wqkv0"][:, 2 * D:3 * D]))
                    load("bv0", vec[:, slot["bv0"], :], a["bqkv0"][2 * D:3 * D].partition_broadcast(P))
            load("wo0", WB[:, :, :], blocks(a["wo0"]))
            load("w10", WC[:, :, :], blocks(a["w10"]))
            for v in VECTORS_0[1:] + ["bias1", "b3"]:
                load_vector(v)
            sp.wait_ge(bias_built, 1)
            load("x", X[:, :, :], blocks(a["x"]))
            wait_full(sp, ("BD", NB - 1))
            load("w12b", W_SD[:, :, :], blocks(a["w12"][:, D:2 * D]))
            wait_full(sp, ("PT", H - 1, NB - 1))
            sp.dma_start(wcn[:, 1, :, :], blocks(a["wn"])).then_inc(loads["wcn"], 16)
            sp.dma_start(wcn[:, 0, :, :], blocks(a["wc"])).then_inc(loads["wcn"], 16)
            for k, w in enumerate(("wq2", "wk2", "wv2")):
                sp.dma_start(wqkv2[:, k, :, :], blocks(a[w])).then_inc(loads["wqkv2"], 16)
            wait_full(sp, ("WO", NB - 1))
            load("wo2", WB[:, :, :], blocks(a["wo2"]))
            load("w3a", WA[:, 1, :, :], blocks(a["w3"][0:D, :]))
            load("w3b", WA[:, 2, :, :], blocks(a["w3"][D:2 * D, :]))
            load("w22", w22, a["w22"].rearrange("(k p) n -> p k n", p=P))
            wait_full(sp, ("W1", NB - 1))
            load("w12a", WC[:, :, :], blocks(a["w12"][:, 0:D]))
            sp.wait_ge(x_ready, NB)
            for v in VECTORS_2:
                load_vector(v)
            for b in range(NB):
                sp.wait_ge(h_ready, 2 * NB + b + 1)
                sp.dma_start(out[b * P:(b + 1) * P, :], HH[:, b, :]).then_inc(out_stored, 16)
            sp.wait_ge(out_stored, 16 * NB)

        @block.gpsimd
        def _(pool):
            steps = [0]

            def link(ins):
                steps[0] += 1
                ins.then_inc(pool_step, 1)
                pool.wait_ge(pool_step, steps[0])

            link(pool.memset(ident[:, :], 0.0))
            pool.affine_select(out=ident[:, :], in_=ident[:, :], compare_op=ALU.not_equal, fill=1.0, base=0,
                               pattern=[[-1, P]], channel_multiplier=1).then_inc(consts, 1)
            pool.memset(ones_row[:, :], 1.0).then_inc(consts, 1)
            pool.memset(eps[:, :], EPS).then_inc(consts, 1)
            pool.iota(iota_n[:, :], pattern=[[1, N]], base=0, channel_multiplier=0,
                      allow_small_or_imprecise_dtypes=True).then_inc(consts, 1)
            pool.iota(iota_w, pattern=[[1, WIN]], base=0, channel_multiplier=0,
                      allow_small_or_imprecise_dtypes=True).then_inc(consts, 1)
            link(pool.memset(later_mask, 1.0))
            pool.affine_select(out=later_mask, in_=later_mask, compare_op=ALU.is_gt, fill=0.0, base=0,
                               pattern=[[1, 2 * P]], channel_multiplier=-1).then_inc(consts, 1)
            pool.memset(A_SD[:, :, :], 0.0).then_inc(zeroed, 1)
            link(pool.memset(W_SD[:, :, :], NEG))
            for b in range(NB):
                pool.affine_select(out=W_SD[:, b, :], in_=W_SD[:, b, :], compare_op=ALU.not_equal, fill=0.0,
                                   base=b * P, pattern=[[-1, N]], channel_multiplier=1).then_inc(diag_set, 1)
            for ap_ in (dstrel[:, NT:NT + 2 * GI], parts[:, NT:NT + 2 * GI, :]):
                pool.memset(ap_, 0.0).then_inc(zeroed, 1)
            pool.iota(window_i[:, :], pattern=[[WIN, NWIN]], base=0, channel_multiplier=0).then_inc(zeroed, 1)
            pool.memset(tr[:, :, NT:NT + 4], 0.0).then_inc(zeroed, 1)

            def add_counts(g, q, base):
                pool.wait_ge(count_ready, g + 1)
                pool.wait_ge(group_added, g + 2)
                win = A_SD[:, :, bass.ds(base, WIN)]
                pool.tensor_tensor(win, win, cnt_g[:, q % 2, :, :], ALU.add).then_inc(group_added, 1)

            pool.wait_ge(base_ready, 1)
            pool.wait_ge(zeroed, 5)
            pool.engine_nop().then_inc(group_added, 2)
            wide = pool.value_load(wide_i[0:1, 0:1], min_val=0, max_val=1)
            with pool.If(wide < 1):
                with pool.Fori(0, NI) as i:
                    for q in range(GI):
                        base = pool.value_load(base_i[0:1, bass.ds(i * GI + q, 1)], min_val=0, max_val=N - WIN)
                        add_counts(i * GI + q, q, base)
            with pool.Else():
                with pool.Fori(0, NWIN) as w:
                    with pool.Fori(0, NI) as i:
                        for q in range(GI):
                            base = pool.value_load(window_i[0:1, bass.ds(w, 1)], min_val=0, max_val=N - WIN)
                            add_counts(w * NG + i * GI + q, q, base)
            pool.engine_nop().then_inc(count_built, 1)

            def resid(out_, x_, vector):
                pool.tensor_tensor(out_, x_, vec[:, slot[vector], :], ALU.add).then_inc(resid_ready, 1)

            pool.wait_ge(bias_built, 1)
            pool.wait_ge(loads["x"], 16)
            pool.wait_ge(loads["bo0"], 16)
            pool.wait_ge(loads["be20"], 16)
            for b in range(NB):
                resid(RB[:, b, :], X[:, b, :], "bo0")
            for b in range(NB):
                resid(QB[:, b, :], X[:, b, :], "be20")
            pool.wait_ge(loads["b10"], 16)
            for b in range(NB):
                pool.wait_ge(h_ready, b + 1)
                resid(RB[:, b, :], HH[:, b, :], "b10")
            pool.wait_ge(loads["bias1"], 16)
            for b in range(NB):
                pool.wait_ge(x_ready, b + 1)
                resid(RB[:, b, :], X[:, b, :], "bias1")
            pool.wait_ge(loads["bo2"], 16)
            for b in range(NB):
                pool.wait_ge(x_ready, NB + b + 1)
                resid(RB[:, b, :], X[:, b, :], "bo2")
            for u in range(NU):
                pool.wait_ge(soft_exp, u + 1)
                if u >= 2:
                    pool.wait_ge(soft_ready, u - 1)
                e, t = sT[:, u % 4, :, :], sum_tree[:, u % 2, :, :]
                link(pool.tensor_tensor(t, e[:, 0:4, :], e[:, 4:8, :], ALU.add))
                link(pool.tensor_tensor(t[:, 0:2, :], t[:, 0:2, :], t[:, 2:4, :], ALU.add))
                pool.tensor_tensor(t[:, 0, :], t[:, 0, :], t[:, 1, :], ALU.add).then_inc(soft_sum, 1)
            pool.wait_ge(loads["be22"], 16)
            pool.wait_ge(out_full, 2 * NB)
            for b in range(NB):
                resid(VB[:, b, :], X[:, b, :], "be22")
            pool.wait_ge(loads["b22"], 16)
            for b in range(NB):
                pool.wait_ge(h_ready, NB + b + 1)
                resid(RB[:, b, :], HH[:, b, :], "b22")
            for b in range(NB):
                pool.wait_ge(x_ready, 2 * NB + b + 1)
                resid(RB[:, b, :], X[:, b, :], "b3")

        @block.scalar
        def _(act):
            act.wait_ge(loads["col"], 16)
            act.activation(q0s[:, 0, :], col[:, 0, :], ACT.Copy, scale=SCALE).then_inc(act_step, 1)
            act.activation(q0s[:, 1, :], col[:, 2, :], ACT.Copy, scale=SCALE).then_inc(act_step, 1)
            act.wait_ge(act_step, 2)

            def evac(name, dst, bias=None, scale=1.0, func=ACT.Identity, src=None):
                wait_full(act, name)
                src = bank_of(name)[:, :] if src is None else src(bank_of(name))
                if bias is None:
                    ins = act.activation(dst, src, ACT.Copy, scale=scale)
                else:
                    ins = act.activation(dst, src, func, bias=bias, scale=scale)
                ins.then_inc(act_emptied, 1)

            def turned(name, dst, b):
                evac(name, dst[:, :, b * P:(b + 1) * P], src=lambda t: t[:, :].rearrange("p (k n) -> p k n", k=NB))

            n_std = [0]

            def std():
                act.wait_ge(stats_ready, n_std[0] + 1)
                k = n_std[0] % 2
                act.activation(sd[:, k, :], mv[:, k, 1:2], ACT.Sqrt, bias=eps[:, :]).then_inc(std_ready, 1)
                n_std[0] += 1

            for b in range(NB):
                evac(("QT", b), QB[:, b, :], bias=q0s[:, 0, b:b + 1], scale=SCALE)
            for b in range(NB):
                evac(("KT", b), KB[:, b, :], bias=col[:, 1, b:b + 1])

            for b in range(NB):
                evac(("V", b), VB[:, b, :])
            for h in range(H):
                for b in range(NB):
                    k = h * NB + b
                    if k % 8 == 0:
                        act.wait_ge(compared, 2 * GI + (k // 8 + 1) * (NT // 4))
                    evac(("S", h, b), probs[:, k, :])

            def take_counts(g, q):
                act.wait_ge(group_full, g + 1)
                act.wait_ge(group_added, g + 1)
                act.activation(cnt_g[:, q % 2, :, :], group_bank[q % 2][:, :, 0, :], ACT.Copy).then_inc(count_ready, 1)

            act.wait_ge(base_ready, 1)
            wide = act.value_load(wide_i[0:1, 0:1], min_val=0, max_val=1)
            with act.If(wide < 1):
                with act.Fori(0, NI) as i:
                    for q in range(GI):
                        take_counts(i * GI + q, q)
            with act.Else():
                with act.Fori(0, NWIN) as w:
                    with act.Fori(0, NI) as i:
                        for q in range(GI):
                            take_counts(w * NG + i * GI + q, q)

            for b in range(NB):
                evac(("AD", b), A_DS[:, b, :])
            def exp0(h, b):
                k = h * NB + b
                act.wait_ge(row_max, k + 1)
                act.activation(probs[:, k, :], probs[:, k, :], ACT.Exp, bias=nmax[:, k:k + 1], scale=-1.0,
                               accum_out=psum_of[:, k:k + 1]).then_inc(exp_done, 1)

            for b in range(NB):
                exp0(0, b)
            for h in range(H):
                for b in range(NB):
                    if h + 1 < H:
                        exp0(h + 1, b)
                    if b % 2 == 0:
                        if b == 0 and h >= 2:
                            act.wait_ge(head_done, h - 1)
                        turned(("PT", h, b), probsT[h % 2], b)
            for b in range(NB):
                turned(("OT", b), XT, b)
            for b in range(NB):
                std()
                turned(("HT", b), XT, b)
            for b in range(NB + 1):
                if b < NB:
                    std()
                    std()
                    turned(("X1T", b), XT, b)
                if b:
                    evac(("BETA", b - 1), KB[:, b - 1, :])
            for b in range(NB):
                std()
            for b in range(NB):
                turned(("X2T", b), XT, b)
            for b in range(NB):
                evac(("KT2", b), KB[:, b, :], bias=col[:, 3, b:b + 1])
            for b in range(NB):
                evac(("QT2", b), QB[:, b, :], bias=q0s[:, 1, b:b + 1], scale=SCALE)

            def exp2(u):
                act.wait_ge(centered, u + 1)
                act.activation(sT[:, u % 4, :, :], sT[:, u % 4, :, :], ACT.Exp).then_inc(soft_exp, 1)

            for u in range(NU):
                if u >= 4:
                    act.wait_ge(head_done, H + u - 4)
                for p in range(H // 2):
                    evac(("ST", u, p), sT[:, u % 4, 2 * p:2 * p + 2, :].rearrange("p h n -> p (h n)"))
                if u:
                    exp2(u - 1)
            exp2(NU - 1)
            for b in range(NB):
                act.wait_ge(out_full, NB + b + 1)
                act.activation(HH[:, b, :], bank[b][:, :], ACT.Copy).then_inc(out_taken, 1)
            for b in range(NB):
                turned(("OT2", b), XT, b)
            for b in range(NB):
                std()
                turned(("HT2", b), XT, b)
            for f in range(2 * NB):
                evac(("FT", f), FT[:, f, :], bias=col[:, 4 + f // NB, f % NB:f % NB + 1], func=ACT.Relu)
            for b in range(NB):
                std()
                std()
                turned(("X3T", b), XT, b)
            for b in range(NB):
                evac(("NST", b), QB[:, b, :])
            for b in range(NB):
                std()

        @block.vector
        def _(dve):
            steps = [0]

            def link(ins):
                steps[0] += 1
                ins.then_inc(dve_step, 1)
                dve.wait_ge(dve_step, steps[0])

            dve.wait_ge(loads["dst"], 16)
            dve.tensor_copy(nat[:, 1, :], dst_i).then_inc(edges_float, 1)
            dve.wait_ge(loads["src"], 16)
            dve.tensor_copy(nat[:, 0, :], src_i).then_inc(edges_float, 1)
            dve.wait_ge(edges_float, 2)
            dve.scalar_tensor_tensor(out=nat[:, 3, :], in0=nat[:, 1, :], scalar=float(N), in1=nat[:, 0, :],
                                     op0=ALU.mult, op1=ALU.add).then_inc(key_ready, 1)
            dve.tensor_reduce(mm[:, 0:1], nat[:, 1, :], AX.X, ALU.min).then_inc(tile_ranges, 1)
            dve.tensor_reduce(mm[:, 1:2], nat[:, 1, :], AX.X, ALU.max).then_inc(tile_ranges, 1)
            dve.wait_ge(ranges_turned, 1)
            link(dve.tensor_copy(row[:, 0:2 * P], bank[3][0:1, 0:2 * P]))
            link(dve.tensor_tensor(row[:, 2 * P:2 * P + NG], row[:, 0:P:2], row[:, 1:P:2], ALU.min))
            link(dve.tensor_tensor(row[:, 3 * P:3 * P + NG], row[:, P:2 * P:2], row[:, P + 1:2 * P:2], ALU.max))
            link(dve.tensor_scalar(base_row[:, 0:NG], row[:, 2 * P:2 * P + NG], float(N - WIN), None, ALU.min))
            link(dve.tensor_copy(base_i[:, :], base_row[:, 0:NG]))
            link(dve.tensor_tensor(row[:, 3 * P:3 * P + NG], row[:, 3 * P:3 * P + NG], base_row[:, 0:NG],
                                   ALU.subtract))
            link(dve.tensor_reduce(base_row[:, NG:NG + 1], row[:, 3 * P:3 * P + NG], AX.X, ALU.max))
            dve.tensor_scalar(wide_i[:, :], base_row[:, NG:NG + 1], float(WIN - 1), None,
                              ALU.is_gt).then_inc(base_ready, 1)
            dve.wait_ge(edges_turned, 1)
            link(dve.tensor_copy(tr[:, :, 0:NT], bank[2][:, :].rearrange("p (k t) -> p k t", k=4)))
            link(dve.tensor_copy(parts[:, 0:NT, 0], ewT[:, 0:NT]))
            link(dve.tensor_tensor(w_rest, ewT[:, 0:NT], parts[:, 0:NT, 0], ALU.subtract))
            link(dve.tensor_copy(parts[:, 0:NT, 1], w_rest))
            link(dve.tensor_tensor(w_rest, w_rest, parts[:, 0:NT, 1], ALU.subtract))
            link(dve.tensor_copy(parts[:, 0:NT, 2], w_rest))
            dve.wait_ge(base_spread, 1)
            link(dve.tensor_copy(base_bc, bank[3][:, 2 * P:2 * P + NG]))
            dve.wait_ge(consts, 6)

            dve.engine_nop().then_inc(compared, 2 * GI)
            for c in range(4):
                dve.wait_ge(loads[f"key{c}"], 16)
                with dve.Fori(0, NI // 4) as i:
                    t0 = i * (2 * GI) + c * (NT // 4)
                    dve.wait_ge(compared, t0 + 2 * GI)
                    for j in range(2 * GI):
                        width = P * (2 - j % 2)
                        dve.scalar_tensor_tensor(
                            out=junk[:, j, 0:width], in0=G[:, bass.ds((t0 + j) * P, width)],
                            scalar=keyT[:, bass.ds(t0 + j, 1)], in1=later_mask[:, 0:width],
                            op0=ALU.is_equal, op1=ALU.mult,
                            accum_out=later[:, bass.ds(t0 + j, 1)]).then_inc(compared, 1)
            dve.wait_ge(compared, NT + 2 * GI)
            link(dve.tensor_scalar(later, later, 0.0, None, ALU.is_equal))
            now = parts[:, 0:NT, :]
            dve.tensor_tensor(now, now, later.rearrange("p (t k) -> p t k", k=1).broadcast_to([P, NT, 3]),
                              ALU.mult).then_inc(flags_done, 1)
            dve.wait_ge(flags_done, 1)
            dve.wait_ge(diag_set, NB)
            dve.wait_ge(zeroed, 5)
            dve.engine_nop().then_inc(group_folded, 2)

            def build_rhs(slot_, i, count):
                t0 = i * 2 * GI
                eq = rhs[:, slot_, :, 0:1, :]
                rel = dstrel[:, bass.ds(t0, 2 * GI)].rearrange("p (t k) -> p t k", k=1)
                w = parts[:, bass.ds(t0, 2 * GI), :].rearrange("p t (k n) -> p t k n", n=1)
                dve.tensor_tensor(rhs[:, slot_, :, 0, :],
                                  iota_w.rearrange("p (k n) -> p k n", k=1).broadcast_to([P, 2 * GI, WIN]),
                                  rel.broadcast_to([P, 2 * GI, WIN]), ALU.is_equal).then_inc(rhs_part, 1)
                dve.wait_ge(rhs_part, count)
                dve.tensor_tensor(rhs[:, slot_, :, 1:4, :], eq.broadcast_to([P, 2 * GI, 3, WIN]),
                                  w.broadcast_to([P, 2 * GI, 3, WIN]), ALU.mult).then_inc(rhs_ready, 1)

            def onehots(t, pair):
                for j in range(2):
                    ins = dve.tensor_scalar(oh[:, pair, j, :], iota_n[:, :], srcT[:, bass.ds(t + j, 1)], None,
                                            ALU.is_equal)
                ins.then_inc(onehot_ready, 1)

            def sweep(g0, r0, base_of):
                build_rhs(0, 0, r0 + 1)
                onehots(0, 0)
                onehots(2, 1)
                with dve.Fori(0, NI // 2) as ii:
                    for s in range(2):
                        i = ii * 2 + s
                        for q in range(GI):
                            g = i * GI + q
                            if q == 1:
                                build_rhs(1 - s, i + 1, r0 + (i + 2))
                            base = base_of(g)
                            win = W_SD[:, :, bass.ds(base, WIN)]
                            onehots(g * 2 + 4, (q + 2) % 4)
                            dve.wait_ge(count_ready, g0 + g + 1)
                            dve.scalar_tensor_tensor(out=win, in0=cnt_g[:, q % 2, :, :], scalar=0.0, in1=win,
                                                     op0=ALU.is_equal, op1=ALU.mult).then_inc(bias_cleared, 1)
                            dve.wait_ge(bias_cleared, g0 + g + 1)
                            dve.tensor_tensor(win, win, group_bank[q % 2][:, :, 1, :],
                                              ALU.add).then_inc(group_folded, 1)
                            dve.wait_ge(group_folded, g0 + g + 3)

            wide = dve.value_load(wide_i[0:1, 0:1], min_val=0, max_val=1)
            with dve.If(wide < 1):
                dve.tensor_tensor(dstrel[:, 0:NT].rearrange("p (g j) -> p g j", j=2),
                                  dstT[:, 0:NT].rearrange("p (g j) -> p g j", j=2),
                                  base_bc.rearrange("p (g j) -> p g j", j=1).broadcast_to([P, NG, 2]),
                                  ALU.subtract).then_inc(dve_step, 1)
                dve.wait_ge(dve_step, steps[0] + 1)
                sweep(0, 0, lambda g: dve.value_load(base_i[0:1, bass.ds(g, 1)], min_val=0, max_val=N - WIN))
            with dve.Else():
                dve.tensor_copy(dstrel[:, 0:NT], dstT[:, 0:NT]).then_inc(dve_step, 1)
                dve.wait_ge(dve_step, steps[0] + 1)
                with dve.Fori(0, NWIN) as w:
                    sweep(w * NG, w * (NI + 1), lambda g: w * WIN)
                    dve.tensor_scalar(dstrel, dstrel, float(WIN), None, ALU.subtract).then_inc(dve_step, 1)
                    dve.wait_ge(dve_step, w + (steps[0] + 2))
            dve.engine_nop().then_inc(bias_built, 1)
            link_sem = sem("dve_link")
            count = [0]

            def link(ins):
                count[0] += 1
                ins.then_inc(link_sem, 1)
                dve.wait_ge(link_sem, count[0])

            for b in range(NB):
                wait_full(dve, ("BD", b))
                dve.tensor_copy(B_DS[:, b, :], bank_of(("BD", b))[:, :]).then_inc(dve_emptied, 1)
            dve.wait_ge(dve_emptied, EMPTIED[("BD", NB - 1)][1])

            def row_least(h, b):
                k = h * NB + b
                dve.tensor_tensor_reduce(out=probs[:, k, :], in0=probs[:, k, :], in1=B_DS[:, b, :],
                                         scale=-1.0, scalar=3.0e38, op0=ALU.add, op1=ALU.min,
                                         accum_out=nmax[:, k:k + 1]).then_inc(row_max, 1)

            wait_emptied(dve, ("S", H - 1, NB - 1))
            for b in range(NB):
                row_least(0, b)
            for h in range(H):
                for b in range(NB):
                    if h + 1 < H:
                        row_least(h + 1, b)
                    if b % 2:
                        if b == 1 and h >= 2:
                            dve.wait_ge(head_done, h - 1)
                        wait_full(dve, ("PT", h, b))
                        dve.tensor_copy(probsT[h % 2][:, :, b * P:(b + 1) * P],
                                        bank_of(("PT", h, b))[:, :].rearrange("p (k n) -> p k n", k=NB)
                                        ).then_inc(dve_emptied, 1)
                if h == 1:
                    dve.wait_ge(count_built, 1)
                    dve.tensor_reduce(cnt_s[:, :], A_SD[:, :, :], AX.X, ALU.add).then_inc(degree_ready, 1)
                    wait_emptied(dve, ("AD", NB - 1))
                    dve.tensor_reduce(cnt_d[:, :], A_DS[:, :, :], AX.X, ALU.add).then_inc(degree_ready, 1)
                    dve.wait_ge(degree_ready, 2)
                    link(dve.reciprocal(rc[:, 0, :], cnt_s[:, :]))
                    link(dve.tensor_scalar(cnt_d[:, :], cnt_d[:, :], 1.0, None, ALU.max))
                    link(dve.reciprocal(rc[:, 1, :], cnt_d[:, :]))
            dve.wait_ge(exp_done, H * NB)
            link(dve.reciprocal(rsum[:, :], psum_of[:, :]))
            by_row = rsum[:, :].rearrange("p (h b) -> p b h", b=NB)
            for b in range(NB):
                dve.wait_ge(out_full, b + 1)
                dve.tensor_tensor(HH[:, b, :].rearrange("p (h d) -> p h d", h=H),
                                  bank[b][:, :].rearrange("p (h d) -> p h d", h=H),
                                  by_row[:, b, :].rearrange("p (h d) -> p h d", d=1).broadcast_to([P, H, HD]),
                                  ALU.mult).then_inc(out_taken, 1)

            n_ln = [0]
            resids = [0]

            def stats(z):
                k = n_ln[0] % 2
                link(dve.bn_stats(st[:, k, 0:6], z))
                dve.bn_aggr(mv[:, k, :], st[:, k, 0:6]).then_inc(stats_ready, 1)
                dve.wait_ge(std_ready, n_ln[0] + 1)
                link(dve.reciprocal(rstd[:, k, :], sd[:, k, :]))
                n_ln[0] += 1
                return mv[:, k, 0:1], rstd[:, k, :]

            def norm(dst, z, done):
                mu, r = stats(z)
                dve.tensor_scalar(dst, z, mu, r, ALU.subtract, ALU.mult).then_inc(done, 1)

            def norm_affine(dst, z, gain, shift, after):
                mu, r = stats(z)
                link(dve.scalar_tensor_tensor(out=z, in0=z, scalar=mu, in1=vec[:, slot[gain], :],
                                              op0=ALU.subtract, op1=ALU.mult))
                return dve.scalar_tensor_tensor(out=dst, in0=z, scalar=r, in1=shift, op0=ALU.mult, op1=ALU.add)

            def take(name, dst, resid):
                wait_full(dve, name)
                dve.tensor_tensor(dst, bank_of(name)[:, :], resid, ALU.add).then_inc(dve_emptied, 1)
                wait_emptied(dve, name)

            def take_scaled(name, dst, scale, resid):
                wait_full(dve, name)
                dve.scalar_tensor_tensor(out=dst, in0=bank_of(name)[:, :], scalar=scale, in1=resid, op0=ALU.mult,
                                         op1=ALU.add).then_inc(dve_emptied, 1)
                wait_emptied(dve, name)

            for v in ("g10", "be10", "g20"):
                dve.wait_ge(loads[v], 16)
            for b in range(NB):
                dve.wait_ge(resid_ready, b + 1)
                take(("WO", b), HH[:, b, :], RB[:, b, :])
                norm_affine(HH[:, b, :], HH[:, b, :], "g10", vec[:, slot["be10"], :], None).then_inc(h_ready, 1)
            for b in range(NB):
                dve.wait_ge(resid_ready, 2 * NB + b + 1)
                take(("W1", b), HH[:, b, :], RB[:, b, :])
                link(norm_affine(X[:, b, :], HH[:, b, :], "g20", QB[:, b, :], None))
                norm(X[:, b, :], X[:, b, :], x_ready)
            for b in range(NB):
                dve.wait_ge(resid_ready, 3 * NB + b + 1)
                take(("ALPHA", b), RB[:, b, :], RB[:, b, :])
            for b in range(NB):
                take_scaled(("SUM", b), HH[:, b, :], rc[:, 0, b:b + 1], RB[:, b, :])
                norm(X[:, b, :], HH[:, b, :], x_ready)
            dve.wait_ge(loads["bv2"], 16)
            for b in range(NB):
                wait_full(dve, ("V2", b))
                dve.tensor_tensor(VB[:, b, :], bank_of(("V2", b))[:, :], vec[:, slot["bv2"], :],
                                  ALU.add).then_inc(dve_emptied, 1)

            def center(u):
                x = sT[:, u % 4, :, :]
                if u:
                    dve.wait_ge(centered, u)
                wait_emptied(dve, ("ST", u, H // 2 - 1))
                link(dve.tensor_tensor(max_tree[:, :, :], x[:, 0:4, :], x[:, 4:8, :], ALU.max))
                link(dve.tensor_tensor(max_tree[:, 0:2, :], max_tree[:, 0:2, :], max_tree[:, 2:4, :], ALU.max))
                link(dve.tensor_tensor(max_tree[:, 0, :], max_tree[:, 0, :], max_tree[:, 1, :], ALU.max))
                dve.tensor_tensor(x, x, max_tree[:, 0:1, :].broadcast_to([P, H, UN]),
                                  ALU.subtract).then_inc(centered, 1)

            def weigh(u):
                e = sT[:, u % 4, :, :]
                edges = A_DS[:, u // 2, u % 2 * UN:(u % 2 + 1) * UN]
                if u >= 2:
                    dve.wait_ge(head_done, H + u - 2)
                dve.tensor_scalar(NADJ[:, u % 2, :], edges, 0.0, 1.0 / H, ALU.is_equal,
                                  ALU.mult).then_inc(notadj_ready, 1)
                dve.wait_ge(soft_sum, u + 1)
                link(dve.reciprocal(share, sum_tree[:, u % 2, 0, :]))
                link(dve.scalar_tensor_tensor(out=share, in0=edges, scalar=0.0, in1=share, op0=ALU.is_gt,
                                              op1=ALU.mult))
                dve.tensor_tensor(e, e, share.rearrange("p (h n) -> p h n", h=1).broadcast_to([P, H, UN]),
                                  ALU.mult).then_inc(soft_ready, 1)
                dve.wait_ge(soft_ready, u + 1)

            for u in range(NU + 2):
                if u < NU:
                    center(u)
                if u >= 2:
                    weigh(u - 2)
            for v in ("g12", "be12", "g22"):
                dve.wait_ge(loads[v], 16)
            for b in range(NB):
                dve.wait_ge(resid_ready, 4 * NB + b + 1)
                take(("WO2", b), HH[:, b, :], RB[:, b, :])
                norm_affine(HH[:, b, :], HH[:, b, :], "g12", vec[:, slot["be12"], :], None).then_inc(h_ready, 1)
            for b in range(NB):
                dve.wait_ge(resid_ready, 6 * NB + b + 1)
                take(("FF", b), HH[:, b, :], RB[:, b, :])
                link(norm_affine(X[:, b, :], HH[:, b, :], "g22", VB[:, b, :], None))
                norm(X[:, b, :], X[:, b, :], x_ready)
            for b in range(NB):
                dve.wait_ge(resid_ready, 7 * NB + b + 1)
                take(("Z1", b), RB[:, b, :], RB[:, b, :])
            for b in range(NB):
                take_scaled(("Z2", b), HH[:, b, :], rc[:, 1, b:b + 1], RB[:, b, :])
                norm(HH[:, b, :], HH[:, b, :], h_ready)

        @block.tensor
        def _(pe):
            def claim(name):
                k = POS[name]
                if k >= R:
                    wait_emptied(pe, ORDER[k - R][0])
                return bank_of(name)

            def product(name, lhs, rhs_, n_k=NB):
                t = claim(name)
                for k in range(n_k):
                    last = nc.tensor.matmul(t[:, :], lhs(k), rhs_(k), start=(k == 0), stop=(k == n_k - 1))
                last.then_inc(ring_full, 1)

            def turn(name, block_of):
                t = claim(name)
                for k in range(NB):
                    last = nc.tensor.transpose(t[:, k * P:(k + 1) * P], block_of(k), ident[:, :])
                last.then_inc(ring_full, 1)

            def cols(t, k, b):
                return t[:, k, b * P:(b + 1) * P]

            pe.wait_ge(consts, 6)
            pe.wait_ge(tile_ranges, 2)
            for k in range(2):
                last = nc.tensor.matmul(bank[3][0:1, k * P:(k + 1) * P], mm[:, k:k + 1], ident[:, :], start=True,
                                        stop=True)
            last.then_inc(ranges_turned, 1)
            pe.wait_ge(loads["ew"], 16)
            for k in range(4):
                last = nc.tensor.transpose(bank[2][:, k * P:(k + 1) * P], nat[:, k, :], ident[:, :])
            last.then_inc(edges_turned, 1)
            pe.wait_ge(base_ready, 1)
            nc.tensor.matmul(bank[3][:, 2 * P:2 * P + NG], ones_row[:, :], base_row[:, 0:NG], start=True,
                             stop=True).then_inc(base_spread, 1)

            pe.wait_ge(loads["xT"], 16)
            pe.wait_ge(loads["wq0"], 16)
            for b in range(NB):
                product(("QT", b), lambda k: cols(WA[:, 0, :, :], k, b), lambda k: XT[:, k, :])
            pe.wait_ge(loads["wk0"], 16)
            for b in range(NB):
                product(("KT", b), lambda k: cols(WA[:, 1, :, :], k, b), lambda k: XT[:, k, :])
            pe.wait_ge(loads["wv0"], 16)
            pe.wait_ge(loads["bv0"], 16)
            for b in range(NB):
                t = claim(("V", b))
                nc.tensor.matmul(t[:, :], ones_row[:, :], vec[0:1, slot["bv0"], :], start=True, stop=False)
                for k in range(NB):
                    last = nc.tensor.matmul(t[:, :], cols(XT, k, b), WA[:, 2, k, :], start=False, stop=(k == NB - 1))
                last.then_inc(ring_full, 1)
            wait_emptied(pe, ("KT", NB - 1))
            for h in range(H):
                r = slice((h % 2) * HD, (h % 2 + 1) * HD)
                for b in range(NB):
                    nc.tensor.matmul(claim(("S", h, b))[:, :], QB[r, h // 2, b * P:(b + 1) * P], KB[r, h // 2, :],
                                     start=True, stop=True).then_inc(ring_full, 1)

            def group(g, oh_count, turn_count, q, s):
                pe.wait_ge(onehot_ready, oh_count)
                pe.wait_ge(rhs_ready, turn_count)
                pe.wait_ge(group_folded, g + 1)
                pe.wait_ge(group_added, g + 1)
                gb = group_bank[q % 2]
                for b in range(NB):
                    for j in range(2):
                        src1 = oh[:, q, j, b * P:(b + 1) * P]
                        t = 2 * q + j
                        nc.tensor.matmul(gb[:, b, :, :], src1, rhs[:, s, t, 0:2, :], start=(j == 0), stop=False)
                        nc.tensor.matmul(gb[:, b, 1, :], src1, rhs[:, s, t, 2, :], start=False, stop=False)
                        last = nc.tensor.matmul(gb[:, b, 1, :], src1, rhs[:, s, t, 3, :], start=False,
                                                stop=(j == 1))
                last.then_inc(group_full, 1)

            wide = pe.value_load(wide_i[0:1, 0:1], min_val=0, max_val=1)
            with pe.If(wide < 1):
                with pe.Fori(0, NI // 2) as ii:
                    for s in range(2):
                        i = ii * 2 + s
                        for q in range(GI):
                            group(i * GI + q, i * GI + (q + 1), i + 1, q, s)
            with pe.Else():
                with pe.Fori(0, NWIN) as w:
                    with pe.Fori(0, NI // 2) as ii:
                        for s in range(2):
                            i = ii * 2 + s
                            for q in range(GI):
                                group(w * NG + i * GI + q, w * (NG + 2) + i * GI + (q + 1), w * (NI + 1) + i + 1, q, s)

            pe.wait_ge(bias_built, 1)
            for b in range(NB):
                turn(("BD", b), lambda k: cols(W_SD, k, b))
            pe.wait_ge(count_built, 1)
            for b in range(NB):
                turn(("AD", b), lambda k: cols(A_SD, k, b))

            wait_emptied(pe, ("V", NB - 1))
            for h in range(H):
                for b in range(NB):
                    pe.wait_ge(exp_done, h * NB + b + 1)
                    turn(("PT", h, b), lambda k: cols(probs, h * NB + b, k))
                wait_emptied(pe, ("PT", h, NB - 2))
                wait_emptied(pe, ("PT", h, NB - 1))
                for b in range(NB):
                    for m in range(NB):
                        last = nc.tensor.matmul(bank[b][:, h * HD:(h + 1) * HD],
                                                probsT[h % 2][:, m, b * P:(b + 1) * P],
                                                VB[:, m, h * HD:(h + 1) * HD], start=(m == 0), stop=(m == NB - 1))
                    if h == H - 1:
                        last.then_inc(out_full, 1)
                if h < H - 1:
                    last.then_inc(head_done, 1)
            for b in range(NB):
                pe.wait_ge(out_taken, b + 1)
                turn(("OT", b), lambda k: cols(HH, b, k))
            pe.wait_ge(loads["wo0"], 16)
            for b in range(NB):
                wait_emptied(pe, ("OT", b))
                product(("WO", b), lambda k: cols(XT, k, b), lambda k: WB[:, k, :])
            pe.wait_ge(loads["w10"], 16)
            for b in range(NB + 1):
                if b < NB:
                    pe.wait_ge(h_ready, b + 1)
                    turn(("HT", b), lambda k: cols(HH, b, k))
                if b:
                    wait_emptied(pe, ("HT", b - 1))
                    product(("W1", b - 1), lambda k: cols(XT, k, b - 1), lambda k: WC[:, k, :])
            pe.wait_ge(loads["wcn"], 32)
            for b in range(NB + 1):
                if b < NB:
                    pe.wait_ge(x_ready, b + 1)
                    turn(("X1T", b), lambda k: cols(X, b, k))
                if b:
                    wait_emptied(pe, ("X1T", b - 1))
                    product(("BETA", b - 1), lambda k: cols(XT, k, b - 1), lambda k: wcn[:, 1, k, :])
                    product(("ALPHA", b - 1), lambda k: cols(XT, k, b - 1), lambda k: wcn[:, 0, k, :])
            wait_emptied(pe, ("BETA", NB - 1))
            for b in range(NB):
                product(("SUM", b), lambda k: cols(A_DS, k, b), lambda k: KB[:, k, :])
            for b in range(NB):
                pe.wait_ge(x_ready, NB + b + 1)
                turn(("X2T", b), lambda k: cols(X, b, k))
            wait_emptied(pe, ("X2T", NB - 1))
            pe.wait_ge(loads["wqkv2"], 48)
            for b in range(NB):
                product(("KT2", b), lambda k: cols(wqkv2[:, 1, :, :], k, b), lambda k: XT[:, k, :])
            for b in range(NB):
                product(("QT2", b), lambda k: cols(wqkv2[:, 0, :, :], k, b), lambda k: XT[:, k, :])
            for b in range(NB):
                product(("V2", b), lambda k: cols(XT, k, b), lambda k: wqkv2[:, 2, k, :])

            def heads_out(u):
                m = u // 2
                pe.wait_ge(notadj_ready, u + 1)
                pe.wait_ge(soft_ready, u + 1)
                for j in range(2):
                    b = u % 2 * 2 + j
                    n = slice(j * P, (j + 1) * P)

                    def others(start, stop):
                        return nc.tensor.matmul(bank[b][:, :], NADJ[:, u % 2, n], VB[:, m, :], start=start,
                                                stop=stop, skip_group_check=True)

                    if m < NB - 1:
                        others(m == 0, False)
                    for i, h in enumerate(UNIT_HEADS):
                        last = nc.tensor.matmul(bank[b][:, h * HD:(h + 1) * HD], sT[:, u % 4, i, n],
                                                VB[:, m, h * HD:(h + 1) * HD], start=False, stop=False,
                                                skip_group_check=True)
                    if m == NB - 1:
                        others(False, True).then_inc(out_full, 1)
                if m < NB - 1:
                    last.then_inc(head_done, 1)

            wait_emptied(pe, ("KT2", NB - 1))
            wait_emptied(pe, ("QT2", NB - 1))
            for u in range(NU + 3):
                if u < NU:
                    m, n = u // 2, slice(u % 2 * UN, (u % 2 + 1) * UN)
                    for p in range(H // 2):
                        t = claim(("ST", u, p))
                        for i, h in enumerate(UNIT_HEADS[2 * p:2 * p + 2]):
                            r = slice((h % 2) * HD, (h % 2 + 1) * HD)
                            last = nc.tensor.matmul(t[:, i * UN:(i + 1) * UN], KB[r, h // 2, m * P:(m + 1) * P],
                                                    QB[r, h // 2, n], start=True, stop=True)
                        last.then_inc(ring_full, 1)
                if u == 3:
                    wait_emptied(pe, ("V2", NB - 1))
                if u >= 3:
                    heads_out(u - 3)
            for b in range(NB):
                pe.wait_ge(out_taken, NB + b + 1)
                turn(("OT2", b), lambda k: cols(HH, b, k))
            pe.wait_ge(loads["wo2"], 16)
            for b in range(NB):
                wait_emptied(pe, ("OT2", b))
                product(("WO2", b), lambda k: cols(XT, k, b), lambda k: WB[:, k, :])
            for b in range(NB):
                pe.wait_ge(h_ready, NB + b + 1)
                turn(("HT2", b), lambda k: cols(HH, b, k))
            wait_emptied(pe, ("HT2", NB - 1))
            pe.wait_ge(loads["w12a"], 16)
            pe.wait_ge(loads["w12b"], 16)
            for f in range(2 * NB):
                w1 = WC if f < NB else W_SD
                product(("FT", f), lambda k: cols(w1, k, f % NB), lambda k: XT[:, k, :])
            wait_emptied(pe, ("FT", 2 * NB - 1))
            pe.wait_ge(loads["w22"], 16)
            for b in range(NB):
                product(("FF", b), lambda k: cols(FT, k, b), lambda k: w22[:, k, :], n_k=2 * NB)
            pe.wait_ge(loads["w3a"], 16)
            for b in range(NB + 1):
                if b < NB:
                    pe.wait_ge(x_ready, 2 * NB + b + 1)
                    turn(("X3T", b), lambda k: cols(X, b, k))
                if b:
                    wait_emptied(pe, ("X3T", b - 1))
                    product(("Z1", b - 1), lambda k: cols(XT, k, b - 1), lambda k: WA[:, 1, k, :])
            for b in range(NB):
                product(("NST", b), lambda k: cols(X, k, b), lambda k: A_SD[:, k, :])
            wait_emptied(pe, ("NST", NB - 1))
            pe.wait_ge(loads["w3b"], 16)
            for b in range(NB):
                product(("Z2", b), lambda k: cols(QB, k, b), lambda k: WA[:, 2, k, :])


def kernel(x, src, dst, edge_weight, L0_gnn_Wqkv, L0_gnn_bqkv, L0_gnn_Wo, L0_gnn_bo, L0_gnn_W1, L0_gnn_b1,
           L0_gnn_g1, L0_gnn_beta1, L0_gnn_g2, L0_gnn_beta2, L1_gnn_wc, L1_gnn_wn, L1_gnn_bias, L2_gnn_Wq,
           L2_gnn_bq, L2_gnn_Wk, L2_gnn_bk, L2_gnn_Wv, L2_gnn_bv, L2_gnn_Wo, L2_gnn_bo, L2_gnn_W1, L2_gnn_b1,
           L2_gnn_W2, L2_gnn_b2, L2_gnn_g1, L2_gnn_be1, L2_gnn_g2, L2_gnn_be2, L3_gnn_W, L3_gnn_b):
    import numpy as np
    import concourse.bacc as bacc
    from concourse.bass_utils import run_bass_kernel_spmd

    def turned(w):
        return np.ascontiguousarray(np.asarray(w).T)

    arrays = {
        "x": x, "xT": turned(x), "src": src, "dst": dst, "ew": edge_weight,
        "wqkv0": turned(L0_gnn_Wqkv), "bqkv0": L0_gnn_bqkv, "wo0": turned(L0_gnn_Wo), "bo0": L0_gnn_bo,
        "w10": turned(L0_gnn_W1), "b10": L0_gnn_b1, "g10": L0_gnn_g1, "be10": L0_gnn_beta1, "g20": L0_gnn_g2,
        "be20": L0_gnn_beta2, "wc": L1_gnn_wc, "wn": L1_gnn_wn, "bias1": L1_gnn_bias,
        "wq2": L2_gnn_Wq, "wk2": L2_gnn_Wk, "wv2": L2_gnn_Wv,
        "bv2": L2_gnn_bv, "wo2": L2_gnn_Wo, "bo2": L2_gnn_bo, "w12": L2_gnn_W1,
        "w22": L2_gnn_W2, "b22": L2_gnn_b2, "g12": L2_gnn_g1, "be12": L2_gnn_be1, "g22": L2_gnn_g2,
        "be22": L2_gnn_be2, "w3": turned(L3_gnn_W), "b3": L3_gnn_b,
    }
    per_feature = [np.asarray(v).reshape(-1, P).T for v in
                   (np.asarray(L0_gnn_bqkv)[:2 * D], L2_gnn_bq, L2_gnn_bk, L2_gnn_b1)]
    arrays["cols"] = np.concatenate(per_feature, axis=1)
    arrays = {f"in_{k}": np.ascontiguousarray(v) for k, v in arrays.items()}
    nc = bacc.Bacc("TRN2", target_bir_lowering=False, num_devices=1)
    aps = {k[3:]: nc.dram_tensor(k, v.shape, mybir.dt.from_np(v.dtype), kind="ExternalInput").ap()
           for k, v in arrays.items()}
    out = nc.dram_tensor("out_x", (N, D), FP32, kind="ExternalOutput").ap()
    gnn_program(nc, aps, out)
    r = run_bass_kernel_spmd(nc, [arrays], core_ids=[0])
    return r.results[0]["out_x"]
```

```python
import concourse.bass as bass
from concourse import mybir
from contextlib import ExitStack

FP32 = mybir.dt.float32
BF16 = mybir.dt.bfloat16
FP16 = mybir.dt.float16
I32 = mybir.dt.int32
ALU = mybir.AluOpType
ACT = mybir.ActivationFunctionType
AX = mybir.AxisListType

P = 128
N = 512
D = 512
NB = N // P
H = 8
HD = D // H
E_ = 16384
NT = E_ // P
NG = NT // 2
WIN = 32
NWIN = N // WIN
GI = 4
NI = NG // GI
KEY_CHUNKS = [0, 1, NI // 4, NI // 2, 3 * NI // 4, NI]
NEG = -1000000000.0
EPS = 1e-05
SCALE = HD ** -0.5
R = 4
NU = 2 * NB
UN = N // 2
UNIT_HEADS = [0, 2, 4, 6, 1, 3, 5, 7]



def ring_order():
    order = []

    def add(stage, index, engine):
        order.append(((stage,) + tuple(index), engine))

    for b in range(NB):
        add("QT", (b,), "A")
    for b in range(NB):
        add("KT", (b,), "A")
    for b in range(NB):
        add("V", (b,), "A")
    for h in range(H):
        for b in range(NB):
            add("S", (h, b), "A")
    for b in range(NB):
        add("BD", (b,), "D")
    for b in range(NB):
        add("AD", (b,), "A")
    for h in range(H):
        for b in range(NB):
            add("PT", (h, b), "AD"[b % 2])
    for b in range(NB):
        add("OT", (b,), "A")
    for b in range(NB):
        add("WO", (b,), "D")
    for b in range(NB + 1):
        if b < NB:
            add("HT", (b,), "A")
        if b:
            add("W1", (b - 1,), "D")
    for b in range(NB + 1):
        if b < NB:
            add("X1T", (b,), "A")
        if b:
            add("BETA", (b - 1,), "A")
            add("ALPHA", (b - 1,), "D")
    for b in range(NB):
        add("SUM", (b,), "D")
    for b in range(NB):
        add("X2T", (b,), "A")
        if b == 2:
            add("V2", (0,), "D")
    for b in range(NB):
        add("KT2", (b,), "A")
    for b in range(NB):
        add("QT2", (b,), "A")
    for u in range(NU):
        for p in range(H // 2):
            add("ST", (u, p), "A")
        if u < NB - 1:
            add("V2", (u + 1,), "D")
    for b in range(NB):
        add("OT2", (b,), "A")
    for b in range(NB):
        add("WO2", (b,), "D")
    for b in range(NB):
        add("HT2", (b,), "A")
    for f in range(2 * NB):
        add("FT", (f,), "A")
    for b in range(NB):
        add("FF", (b,), "D")
    for b in range(NB + 1):
        if b < NB:
            add("X3T", (b,), "A")
        if b:
            add("Z1", (b - 1,), "D")
    for b in range(NB):
        add("NST", (b,), "A")
    for b in range(NB):
        add("Z2", (b,), "D")
    return order


ORDER = ring_order()
POS = {name: k for k, (name, _) in enumerate(ORDER)}
EMPTIED = {}
for _k, (_name, _engine) in enumerate(ORDER):
    EMPTIED[_name] = (_engine, 1 + sum(e == _engine for _, e in ORDER[:_k]))

VECTORS_0 = ["bv0", "bo0", "b10", "g10", "be10", "g20", "be20"]
VECTORS_2 = ["bv2", "bo2", "b22", "g12", "be12", "g22", "be22"]


def gnn_program(nc, a, out):
    ctx = ExitStack()
    with ctx:
        def sb(name, shape, dt=FP32):
            return ctx.enter_context(nc.sbuf_tensor(name, shape, dt))

        def sem(name):
            return ctx.enter_context(nc.semaphore(name))

        key_dram = nc.dram_tensor("key_scratch", [NT, P], FP32, kind="Internal").ap()

        X = sb("X", [P, NB, D])
        HH = sb("HH", [P, NB, D])
        RB = sb("RB", [P, NB, D])
        QB = sb("QB", [P, NB, N])
        KB = sb("KB", [P, NB, N])
        VB = sb("VB", [P, NB, D])
        WAF = sb("WAF", [P, 4 * NB * D + 2 * GI * 2 * WIN])
        WA = WAF[:, 0:4 * NB * D].rearrange("p (w b n) -> p w b n", w=4, b=NB)
        XT = WA[:, 3, :, :]
        rhs = WAF[:, :].bitcast(BF16).rearrange("p (t k n) -> p t k n", t=NT + 2 * GI, k=4)
        WB = sb("WB", [P, NB, D])
        WC = sb("WC", [P, NB, D])
        A_SD = sb("A_SD", [P, NB, N])
        W_SD = sb("W_SD", [P, NB, N])
        G = sb("G", [P, E_])
        probs = G[:, :].rearrange("p (k n) -> p k n", n=N)
        wqk2 = G[:, 0:4096].rearrange("p (w k n) -> p w k n", w=2, k=NB)
        wcn = G[:, 8192:12288].rearrange("p (w k n) -> p w k n", w=2, k=NB)
        w22 = G[:, 12288:16384].rearrange("p (k n) -> p k n", k=2 * NB)
        sT = G[:, 0:8192].rearrange("p (s h n) -> p s h n", s=4, h=H)
        max_tree = G[:, 8192:9216].rearrange("p (h n) -> p h n", h=4)
        sum_tree = G[:, 9216:11264].rearrange("p (s h n) -> p s h n", s=2, h=4)
        share = G[:, 11264:11520]
        NADJ = HH
        FT = G[:, 0:4096].rearrange("p (f n) -> p f n", f=2 * NB)
        A_DS = WA[:, 0, :, :]
        B_DS = WA[:, 1, :, :]
        probsT = [XT, WA[:, 2, :, :]]
        vec = sb("vec", [P, 9, D])
        col = sb("col", [P, 6, NB])
        q0s = sb("q0s", [P, 2, NB])
        ident = sb("ident", [P, P])
        ones_row = sb("ones_row", [1, P])
        eps = sb("eps", [P, 1])
        st = sb("st", [P, 2, 8])
        mv = sb("mv", [P, 2, 2])
        sd = sb("sd", [P, 2, 1])
        rstd = sb("rstd", [P, 2, 1])
        nmax = sb("nmax", [P, H * NB])
        row_sums = sb("row_sums", [P, H * NB])
        inverse_sums = sb("inverse_sums", [P, H * NB])
        cnt_s = sb("cnt_s", [P, NB])
        cnt_d = sb("cnt_d", [P, NB])
        rc = sb("rc", [P, 2, NB])
        base_row = sb("base_row", [1, NG + 8])
        base_i = sb("base_i", [1, NG], I32)
        packed_i = sb("packed_i", [1, NI], I32)
        window_i = sb("window_i", [1, NWIN], I32)
        wide_i = sb("wide_i", [1, 1], I32)
        row = sb("row", [1, 4 * P])
        hf = HH[:, :, :].rearrange("p b n -> p (b n)")
        src_i = hf[:, 0:128].bitcast(I32)
        dst_i = hf[:, 128:256].bitcast(I32)
        nat = hf[:, 256:768].rearrange("p (k e) -> p k e", k=4)
        tr = sb("tr", [P, 4, NT + 2 * GI])
        minus_src = sb("minus_src", [P, NT + 2 * GI])
        srcT, dstT, ewT, keyT = (tr[:, k, :] for k in range(4))
        later_mask = hf[:, 768:1024]
        later = hf[:, 1024:1152]
        w_rest = hf[:, 1152:1280]
        dstrel = hf[:, 1280:1280 + NT]
        parts = hf[:, 1408:1408 + 3 * NT // 2].bitcast(BF16).rearrange("p (t k) -> p t k", k=3)
        iota_w = hf[:, 1620:1636].bitcast(FP16)
        mm = hf[:, 1636:1638]
        base_bc = hf[:, 1638:1638 + NG]
        one = sb("one", [P, 1])
        rhs_now = sb("rhs_now", [P, GI, 2, 4, WIN], BF16)
        rf = RB[:, :, :].rearrange("p b n -> p (b n)")
        junk = rf[:, 0:1024].bitcast(BF16).rearrange("p (s e) -> p s e", s=2 * GI)
        distance = rf[:, 1024:1024 + (GI - 1) * N // 2].bitcast(FP16).rearrange("p (q n) -> p q n", q=GI - 1)
        oh = X[:, :, :].rearrange("p b n -> p (b n)").bitcast(BF16).rearrange("p (g t n) -> p g t n", g=4, t=2)
        iota_n = sb("iota_n", [P, N], FP16)
        cnt_g = hf[:, 256:768].rearrange("p (q b n) -> p q b n", q=GI, b=NB)

        bank = [ctx.enter_context(nc.psum_tensor(f"bank{i}", [P, 512], FP32)) for i in range(8)]
        ring = bank[4:8]
        group_bank = [bank[i][:, 0:NB * 2 * WIN].rearrange("p (b k n) -> p b k n", b=NB, k=2) for i in range(GI)]

        loads = {}

        def load_sem(name):
            loads[name] = sem("ld_" + name)
            return loads[name]

        ring_full = sem("ring_full")
        act_emptied = sem("act_emptied")
        dve_emptied = sem("dve_emptied")
        key_ready = sem("key_ready")
        key_stored = sem("key_stored")
        edges_float = sem("edges_float")
        tile_ranges = sem("tile_ranges")
        edges_turned = sem("edges_turned")
        ranges_turned = sem("ranges_turned")
        base_ready = sem("base_ready")
        base_spread = sem("base_spread")
        consts = sem("consts")
        zeroed = sem("zeroed")
        diag_set = sem("diag_set")
        compared = sem("compared")
        flags_done = sem("flags_done")
        dst_relative = sem("dst_relative")
        src_turned = sem("src_turned")
        windows_ready = sem("windows_ready")
        rhs_pool = sem("rhs_pool")
        rhs_dve = sem("rhs_dve")
        renewed = sem("renewed")
        onehot_act = sem("onehot_act")
        distance_ready = sem("distance_ready")
        rebuild_step = sem("rebuild_step")
        group_full = sem("group_full")
        count_ready = sem("count_ready")
        bias_cleared = sem("bias_cleared")
        group_folded = sem("group_folded")
        group_added = sem("group_added")
        bias_built = sem("bias_built")
        count_built = sem("count_built")
        dve_step = sem("dve_step")
        act_step = sem("act_step")
        pool_step = sem("pool_step")
        row_max = sem("row_max")
        exp_done = sem("exp_done")
        out_full = sem("out_full")
        head_done = sem("head_done")
        out_taken = sem("out_taken")
        stats_ready = sem("stats_ready")
        std_ready = sem("std_ready")
        h_ready = sem("h_ready")
        x_ready = sem("x_ready")
        values_ready = sem("values_ready")
        resid_ready = sem("resid_ready")
        degree_ready = sem("degree_ready")
        centered = sem("centered")
        soft_exp = sem("soft_exp")
        soft_sum = sem("soft_sum")
        soft_ready = sem("soft_ready")
        log_ready = sem("log_ready")
        inverse_ready = sem("inverse_ready")
        notadj_ready = sem("notadj_ready")
        out_stored = sem("out_stored")

        block = ctx.enter_context(nc.Block())

        def wait_emptied(eng, name):
            engine, count = EMPTIED[name]
            eng.wait_ge(act_emptied if engine == "A" else dve_emptied, count)

        def wait_full(eng, name):
            eng.wait_ge(ring_full, POS[name] + 1)

        def bank_of(name):
            return ring[POS[name] % R]

        def blocks(w):
            return w.rearrange("(k p) n -> p k n", p=P)

        all_loads = ["src", "dst", "ew", "wk0", "wv0", "x", "wo0", "w10", "wcn", "bias1", "b3",
                     "col", "wqk2", "wv2", "wo2", "w12a", "w12b", "w22", "w3a", "w3b"] + VECTORS_0 + VECTORS_2 + \
                    [f"key{c}" for c in range(len(KEY_CHUNKS) - 1)]
        all_loads += [f"{name}_{k}" for name in ("xT", "wq0") for k in range(NB)]
        for name in all_loads:
            load_sem(name)
        slot = {v: i for i, v in enumerate(VECTORS_0)} | {v: i for i, v in enumerate(VECTORS_2)} | \
            {"bias1": 7, "b3": 8}

        @block.sync
        def _(sp):
            def load(name, dst, src):
                sp.dma_start(dst, src).then_inc(loads[name], 16)

            def load_vector(name):
                load(name, vec[:, slot[name], :], a[name].partition_broadcast(P))

            load("dst", dst_i, a["dst"].rearrange("(t e) -> t e", e=P))
            load("src", src_i, a["src"].rearrange("(t e) -> t e", e=P))
            load("ew", nat[:, 2, :], a["ew"].rearrange("(t e) -> t e", e=P))
            for k in range(NB):
                load(f"xT_{k}", XT[:, k, :], a["xT"][k * P:(k + 1) * P, :])
                load(f"wq0_{k}", WA[:, 0, k, :], a["wqkv0"][k * P:(k + 1) * P, 0:D])
            load("col", col[:, :, :], a["cols"].rearrange("p (g k) -> p g k", k=NB))
            sp.wait_ge(key_ready, 1)
            sp.dma_start(key_dram, nat[:, 3, :]).then_inc(key_stored, 16)
            sp.wait_ge(key_stored, 16)
            flat = key_dram.rearrange("t e -> (t e)")
            for c in range(len(KEY_CHUNKS) - 1):
                part = slice(KEY_CHUNKS[c] * 2 * GI * P, KEY_CHUNKS[c + 1] * 2 * GI * P)
                load(f"key{c}", G[:, part], flat[part].partition_broadcast(P))
                if c == 0:
                    load("wk0", WA[:, 1, :, :], blocks(a["wqkv0"][:, D:2 * D]))
                if c == 1:
                    load("wv0", WA[:, 2, :, :], blocks(a["wqkv0"][:, 2 * D:3 * D]))
                    load("bv0", vec[:, slot["bv0"], :], a["bqkv0"][2 * D:3 * D].partition_broadcast(P))
            load("wo0", WB[:, :, :], blocks(a["wo0"]))
            load("w10", WC[:, :, :], blocks(a["w10"]))
            for v in VECTORS_0[1:] + ["bias1", "b3"]:
                load_vector(v)
            sp.wait_ge(bias_built, 1)
            load("x", X[:, :, :], blocks(a["x"]))
            wait_full(sp, ("BD", NB - 1))
            load("w12b", W_SD[:, :, :], blocks(a["w12"][:, D:2 * D]))
            wait_full(sp, ("PT", H - 1, NB - 1))
            sp.dma_start(wcn[:, 1, :, :], blocks(a["wn"])).then_inc(loads["wcn"], 16)
            sp.dma_start(wcn[:, 0, :, :], blocks(a["wc"])).then_inc(loads["wcn"], 16)
            for k, w in enumerate(("wq2", "wk2")):
                sp.dma_start(wqk2[:, k, :, :], blocks(a[w])).then_inc(loads["wqk2"], 16)
            wait_full(sp, ("WO", NB - 1))
            load("wo2", WB[:, :, :], blocks(a["wo2"]))
            load("w3a", WA[:, 1, :, :], blocks(a["w3"][0:D, :]))
            load("w3b", WA[:, 2, :, :], blocks(a["w3"][D:2 * D, :]))
            load("w22", w22, a["w22"].rearrange("(k p) n -> p k n", p=P))
            wait_full(sp, ("W1", NB - 1))
            load("wv2", WC[:, :, :], blocks(a["wv2"]))
            sp.wait_ge(x_ready, NB)
            for v in VECTORS_2:
                load_vector(v)
            wait_full(sp, ("V2", NB - 1))
            load("w12a", WC[:, :, :], blocks(a["w12"][:, 0:D]))
            for b in range(NB):
                sp.wait_ge(h_ready, 2 * NB + b + 1)
                sp.dma_start(out[b * P:(b + 1) * P, :], HH[:, b, :]).then_inc(out_stored, 16)
            sp.wait_ge(out_stored, 16 * NB)

        def tiles_of(c):
            return slice(0, NT) if c is None else slice(c * NT // 4, (c + 1) * NT // 4)

        def windows(eng, c, done=windows_ready):
            n = tiles_of(c).stop - tiles_of(c).start
            eng.tensor_tensor(rhs[:, tiles_of(c), 0, :],
                              iota_w.rearrange("p (k n) -> p k n", k=1).broadcast_to([P, n, WIN]),
                              dstrel[:, tiles_of(c)].rearrange("p (t k) -> p t k", k=1).broadcast_to([P, n, WIN]),
                              ALU.is_equal).then_inc(done, 1)

        def weights(eng, c, done):
            t = tiles_of(c)
            n = t.stop - t.start
            if c is not None:
                eng.wait_ge(windows_ready, c + 1)
                eng.wait_ge(flags_done, c + 1)
            eng.tensor_tensor(rhs[:, t, 1:4, :], rhs[:, t, 0:1, :].broadcast_to([P, n, 3, WIN]),
                              parts[:, t, :].rearrange("p t (k n) -> p t k n", n=1).broadcast_to([P, n, 3, WIN]),
                              ALU.mult).then_inc(done, 1)

        @block.gpsimd
        def _(pool):
            steps = [0]

            def link(ins):
                steps[0] += 1
                ins.then_inc(pool_step, 1)
                pool.wait_ge(pool_step, steps[0])

            link(pool.memset(ident[:, :], 0.0))
            pool.affine_select(out=ident[:, :], in_=ident[:, :], compare_op=ALU.not_equal, fill=1.0, base=0,
                               pattern=[[-1, P]], channel_multiplier=1).then_inc(consts, 1)
            pool.memset(ones_row[:, :], 1.0).then_inc(consts, 1)
            pool.memset(eps[:, :], EPS).then_inc(consts, 1)
            pool.memset(one[:, :], 1.0).then_inc(consts, 1)
            pool.iota(iota_n[:, :], pattern=[[1, N]], base=0, channel_multiplier=0,
                      allow_small_or_imprecise_dtypes=True).then_inc(consts, 1)
            pool.iota(iota_w, pattern=[[1, WIN]], base=0, channel_multiplier=0,
                      allow_small_or_imprecise_dtypes=True).then_inc(consts, 1)
            link(pool.memset(later_mask, 1.0))
            pool.affine_select(out=later_mask, in_=later_mask, compare_op=ALU.is_gt, fill=0.0, base=0,
                               pattern=[[1, 2 * P]], channel_multiplier=-1).then_inc(consts, 1)
            pool.memset(A_SD[:, :, :], 0.0).then_inc(zeroed, 1)
            link(pool.memset(W_SD[:, :, :], NEG))
            for b in range(NB):
                pool.affine_select(out=W_SD[:, b, :], in_=W_SD[:, b, :], compare_op=ALU.not_equal, fill=0.0,
                                   base=b * P, pattern=[[-1, N]], channel_multiplier=1).then_inc(diag_set, 1)
            pool.iota(window_i[:, :], pattern=[[WIN, NWIN]], base=0, channel_multiplier=0).then_inc(zeroed, 1)
            pool.memset(rhs[:, NT:NT + 2 * GI, :, :], 0.0).then_inc(zeroed, 1)
            pool.wait_ge(consts, 7)
            pool.wait_ge(src_turned, 1)

            pool.wait_ge(loads["bv0"], 16)
            for c in range(3):
                if c == 2:
                    wait_emptied(pool, ("V", NB - 1))
                    for b in range(NB):
                        pool.tensor_tensor(VB[:, b, :], VB[:, b, :], vec[:, slot["bv0"], :],
                                           ALU.add).then_inc(values_ready, 1)
                weights(pool, c, rhs_pool)

            def add_counts(g, q, base):
                pool.wait_ge(count_ready, g + 1)
                pool.wait_ge(group_added, g + GI)
                win = A_SD[:, :, bass.ds(base, WIN)]
                pool.tensor_tensor(win, win, cnt_g[:, q, :, :], ALU.add).then_inc(group_added, 1)

            pool.wait_ge(base_ready, 1)
            pool.wait_ge(zeroed, 3)
            pool.engine_nop().then_inc(group_added, GI)
            wide = pool.value_load(wide_i[0:1, 0:1], min_val=0, max_val=1)
            with pool.If(wide < 1):
                with pool.Fori(0, NI) as i:
                    for q in range(GI):
                        base = pool.value_load(base_i[0:1, bass.ds(i * GI + q, 1)], min_val=0, max_val=N - WIN)
                        add_counts(i * GI + q, q, base)
            with pool.Else():
                with pool.Fori(0, NWIN) as w:
                    with pool.Fori(0, NI) as i:
                        for q in range(GI):
                            base = pool.value_load(window_i[0:1, bass.ds(w, 1)], min_val=0, max_val=N - WIN)
                            add_counts(w * NG + i * GI + q, q, base)
            pool.engine_nop().then_inc(count_built, 1)

            def resid(out_, x_, vector):
                pool.tensor_tensor(out_, x_, vec[:, slot[vector], :], ALU.add).then_inc(resid_ready, 1)

            pool.wait_ge(bias_built, 1)
            pool.wait_ge(loads["x"], 16)
            pool.wait_ge(loads["bo0"], 16)
            pool.wait_ge(loads["be20"], 16)
            for b in range(NB):
                resid(RB[:, b, :], X[:, b, :], "bo0")
            for b in range(NB):
                resid(QB[:, b, :], X[:, b, :], "be20")
            pool.wait_ge(loads["b10"], 16)
            for b in range(NB):
                pool.wait_ge(h_ready, b + 1)
                resid(RB[:, b, :], HH[:, b, :], "b10")
            pool.wait_ge(loads["bias1"], 16)
            for b in range(NB):
                pool.wait_ge(x_ready, b + 1)
                resid(RB[:, b, :], X[:, b, :], "bias1")
            pool.wait_ge(loads["bo2"], 16)
            for b in range(NB):
                pool.wait_ge(x_ready, NB + b + 1)
                resid(RB[:, b, :], X[:, b, :], "bo2")
            for b in range(NB):
                pool.tensor_scalar(NADJ[:, b, :], A_DS[:, b, :], 0.0, 1.0 / H, ALU.is_equal,
                                   ALU.mult).then_inc(notadj_ready, 1)
            for u in range(NU):
                pool.wait_ge(soft_exp, u + 1)
                if u >= 2:
                    pool.wait_ge(soft_ready, u - 1)
                e, t = sT[:, u % 4, :, :], sum_tree[:, u % 2, :, :]
                link(pool.tensor_tensor(t, e[:, 0:4, :], e[:, 4:8, :], ALU.add))
                link(pool.tensor_tensor(t[:, 0:2, :], t[:, 0:2, :], t[:, 2:4, :], ALU.add))
                pool.tensor_tensor(t[:, 0, :], t[:, 0, :], t[:, 1, :], ALU.add).then_inc(soft_sum, 1)
            pool.wait_ge(loads["be22"], 16)
            pool.wait_ge(out_full, 2 * NB)
            for b in range(NB):
                resid(VB[:, b, :], X[:, b, :], "be22")
            pool.wait_ge(loads["b22"], 16)
            for b in range(NB):
                pool.wait_ge(h_ready, NB + b + 1)
                resid(RB[:, b, :], HH[:, b, :], "b22")
            for b in range(NB):
                pool.wait_ge(x_ready, 2 * NB + b + 1)
                resid(RB[:, b, :], X[:, b, :], "b3")

        @block.scalar
        def _(act):
            act.wait_ge(loads["col"], 16)
            act.activation(q0s[:, 0, :], col[:, 0, :], ACT.Copy, scale=SCALE).then_inc(act_step, 1)
            act.activation(q0s[:, 1, :], col[:, 2, :], ACT.Copy, scale=SCALE).then_inc(act_step, 1)
            act.wait_ge(act_step, 2)

            def evac(name, dst, bias=None, scale=1.0, func=ACT.Identity, src=None):
                wait_full(act, name)
                src = bank_of(name)[:, :] if src is None else src(bank_of(name))
                if bias is None:
                    ins = act.activation(dst, src, ACT.Copy, scale=scale)
                else:
                    ins = act.activation(dst, src, func, bias=bias, scale=scale)
                ins.then_inc(act_emptied, 1)

            def turned(name, dst, b):
                evac(name, dst[:, :, b * P:(b + 1) * P], src=lambda t: t[:, :].rearrange("p (k n) -> p k n", k=NB))

            n_std = [0]

            def std():
                act.wait_ge(stats_ready, n_std[0] + 1)
                k = n_std[0] % 2
                act.activation(sd[:, k, :], mv[:, k, 1:2], ACT.Sqrt, bias=eps[:, :]).then_inc(std_ready, 1)
                n_std[0] += 1

            def norms_ahead(b, n):
                for _ in range(n if b + 1 < NB else 0):
                    std()

            for b in range(NB):
                evac(("QT", b), QB[:, b, :], bias=q0s[:, 0, b:b + 1], scale=SCALE)
            for b in range(NB):
                evac(("KT", b), KB[:, b, :], bias=col[:, 1, b:b + 1])

            def groups(q):
                return 2 if q == GI - 2 else 1

            def src_distance(t, q):
                act.activation(distance[:, q, :], iota_n[:, :], ACT.Abs, bias=minus_src[:, bass.ds(t, 1)]).then_inc(
                    distance_ready, groups(q))

            def src_onehot(count, q):
                act.wait_ge(distance_ready, count)
                act.activation(oh[:, q, 1, :], distance[:, q, :], ACT.Relu, bias=one[:, :],
                               scale=-1.0).then_inc(onehot_act, groups(q))

            act.wait_ge(src_turned, 2)
            act.wait_ge(consts, 7)
            for q in range(GI - 1):
                src_distance(2 * q + 1, q)
                src_onehot(q + 1, q)
            for b in range(NB):
                evac(("V", b), VB[:, b, :])
            for h in range(H):
                for b in range(NB):
                    k = h * NB + b
                    if k % 8 == 0:
                        act.wait_ge(compared, 2 * GI + (k // 8 + 1) * (NT // 4))
                    evac(("S", h, b), probs[:, k, :])

            def take_counts(g, t_next, q):
                act.wait_ge(group_full, g + 1)
                act.wait_ge(group_added, g + 1)
                act.activation(cnt_g[:, q, :, :], group_bank[q][:, :, 0, :], ACT.Copy).then_inc(count_ready, 1)
                if q < GI - 1:
                    src_distance(t_next, q)
                    src_onehot(g + (GI + 1), q)

            act.wait_ge(base_ready, 1)
            wide = act.value_load(wide_i[0:1, 0:1], min_val=0, max_val=1)
            with act.If(wide < 1):
                with act.Fori(0, NG, GI) as g0:
                    g0 = g0.with_bounds(max_val=NG - GI)
                    for q in range(GI):
                        take_counts(g0 + q, g0 * 2 + (2 * GI + 2 * q + 1), q)
            with act.Else():
                with act.Fori(0, NWIN) as w:
                    with act.Fori(0, NG, GI) as g0:
                        g0 = g0.with_bounds(max_val=NG - GI)
                        for q in range(GI):
                            take_counts(w * NG + g0 + q, g0 * 2 + (2 * GI + 2 * q + 1), q)

            for b in range(NB):
                evac(("AD", b), A_DS[:, b, :])
            def exp0(h, b):
                k = h * NB + b
                act.wait_ge(row_max, k + 1)
                act.activation(probs[:, k, :], probs[:, k, :], ACT.Exp, bias=nmax[:, k:k + 1], scale=-1.0,
                               accum_out=row_sums[:, k:k + 1]).then_inc(exp_done, 1)

            for b in range(NB):
                exp0(0, b)
            for h in range(H):
                for b in range(NB):
                    if h + 1 < H:
                        exp0(h + 1, b)
                    if b % 2 == 0:
                        if b == 0 and h >= 2:
                            act.wait_ge(head_done, h - 1)
                        turned(("PT", h, b), probsT[h % 2], b)
            for b in range(NB):
                turned(("OT", b), XT, b)
            std()
            for b in range(NB):
                norms_ahead(b, 1)
                turned(("HT", b), XT, b)
            std()
            std()
            for b in range(NB + 1):
                if b < NB:
                    norms_ahead(b, 2)
                    turned(("X1T", b), XT, b)
                if b:
                    evac(("BETA", b - 1), KB[:, b - 1, :])
            for b in range(NB):
                std()
            for b in range(NB):
                turned(("X2T", b), XT, b)
            for b in range(NB):
                evac(("KT2", b), KB[:, b, :], bias=col[:, 3, b:b + 1])
            for b in range(NB):
                evac(("QT2", b), QB[:, b, :], bias=q0s[:, 1, b:b + 1], scale=SCALE)

            def exp2(u):
                act.wait_ge(centered, u + 1)
                act.activation(sT[:, u % 4, :, :], sT[:, u % 4, :, :], ACT.Exp).then_inc(soft_exp, 1)

            act.preload_act_table_set("natural_log_exp_and_others")

            def invert(u):
                act.wait_ge(soft_sum, u + 1)
                act.activation(sum_tree[:, u % 2, 3, :], sum_tree[:, u % 2, 0, :], ACT.Ln).then_inc(log_ready, 1)
                act.wait_ge(log_ready, u + 1)
                act.activation(sum_tree[:, u % 2, 3, :], sum_tree[:, u % 2, 3, :], ACT.Exp,
                               scale=-1.0).then_inc(inverse_ready, 1)

            for u in range(NU):
                if u >= 4:
                    act.wait_ge(head_done, H + u - 4)
                for p in range(H // 2):
                    evac(("ST", u, p), sT[:, u % 4, 2 * p:2 * p + 2, :].rearrange("p h n -> p (h n)"))
                    if p == 1 and u:
                        exp2(u - 1)
                    if p == 3 and u > 1:
                        invert(u - 2)
            exp2(NU - 1)
            invert(NU - 2)
            invert(NU - 1)
            for b in range(NB):
                act.wait_ge(out_full, NB + b + 1)
                act.activation(HH[:, b, :], bank[b][:, :], ACT.Copy).then_inc(out_taken, 1)
            for b in range(NB):
                turned(("OT2", b), XT, b)
            std()
            for b in range(NB):
                norms_ahead(b, 1)
                turned(("HT2", b), XT, b)
            for f in range(2 * NB):
                evac(("FT", f), FT[:, f, :], bias=col[:, 4 + f // NB, f % NB:f % NB + 1], func=ACT.Relu)
            std()
            std()
            for b in range(NB):
                norms_ahead(b, 2)
                turned(("X3T", b), XT, b)
            for b in range(NB):
                evac(("NST", b), QB[:, b, :])
            for b in range(NB):
                std()

        @block.vector
        def _(dve):
            steps = [0]

            def link(ins):
                steps[0] += 1
                ins.then_inc(dve_step, 1)
                dve.wait_ge(dve_step, steps[0])

            dve.wait_ge(loads["dst"], 16)
            dve.tensor_copy(nat[:, 1, :], dst_i).then_inc(edges_float, 1)
            dve.wait_ge(loads["src"], 16)
            dve.tensor_copy(nat[:, 0, :], src_i).then_inc(edges_float, 1)
            dve.wait_ge(edges_float, 2)
            dve.scalar_tensor_tensor(out=nat[:, 3, :], in0=nat[:, 1, :], scalar=float(N), in1=nat[:, 0, :],
                                     op0=ALU.mult, op1=ALU.add).then_inc(key_ready, 1)
            dve.tensor_reduce(mm[:, 0:1], nat[:, 1, :], AX.X, ALU.min).then_inc(tile_ranges, 1)
            dve.tensor_reduce(mm[:, 1:2], nat[:, 1, :], AX.X, ALU.max).then_inc(tile_ranges, 1)
            dve.wait_ge(ranges_turned, 1)
            link(dve.tensor_copy(row[:, 0:2 * P], bank[3][0:1, 0:2 * P]))
            link(dve.tensor_tensor(row[:, 2 * P:2 * P + NG], row[:, 0:P:2], row[:, 1:P:2], ALU.min))
            link(dve.tensor_tensor(row[:, 3 * P:3 * P + NG], row[:, P:2 * P:2], row[:, P + 1:2 * P:2], ALU.max))
            link(dve.tensor_scalar(base_row[:, 0:NG], row[:, 2 * P:2 * P + NG], float(N - WIN), None, ALU.min))
            link(dve.tensor_copy(base_i[:, :], base_row[:, 0:NG]))
            link(dve.tensor_scalar(base_i[:, :], base_i[:, :], 2, None, ALU.logical_shift_right))
            quarter = base_i[:, :].rearrange("p (i q) -> p i q", q=GI)
            link(dve.tensor_copy(packed_i[:, :], quarter[:, :, GI - 1]))
            for q in reversed(range(GI - 1)):
                link(dve.tensor_scalar(packed_i[:, :], packed_i[:, :], 7, None, ALU.logical_shift_left))
                link(dve.tensor_tensor(packed_i[:, :], packed_i[:, :], quarter[:, :, q], ALU.bitwise_or))
            link(dve.tensor_scalar(base_i[:, :], base_i[:, :], 2, None, ALU.logical_shift_left))
            link(dve.tensor_copy(base_row[:, 0:NG], base_i[:, :]))
            link(dve.tensor_tensor(row[:, 3 * P:3 * P + NG], row[:, 3 * P:3 * P + NG], base_row[:, 0:NG],
                                   ALU.subtract))
            link(dve.tensor_reduce(base_row[:, NG:NG + 1], row[:, 3 * P:3 * P + NG], AX.X, ALU.max))
            dve.tensor_scalar(wide_i[:, :], base_row[:, NG:NG + 1], float(WIN - 1), None,
                              ALU.is_gt).then_inc(base_ready, 1)
            dve.wait_ge(edges_turned, 1)
            link(dve.tensor_copy(tr[:, :, 0:NT], bank[2][:, :].rearrange("p (k t) -> p k t", k=4)))
            link(dve.tensor_copy(srcT[:, NT:NT + 2 * GI], srcT[:, 0:2 * GI]))
            dve.tensor_scalar(minus_src[:, :], srcT, -1.0, None, ALU.mult).then_inc(src_turned, 1)
            dve.engine_nop().then_inc(src_turned, 1)
            link(dve.tensor_copy(parts[:, 0:NT, 0], ewT[:, 0:NT]))
            link(dve.tensor_tensor(w_rest, ewT[:, 0:NT], parts[:, 0:NT, 0], ALU.subtract))
            link(dve.tensor_copy(parts[:, 0:NT, 1], w_rest))
            link(dve.tensor_tensor(w_rest, w_rest, parts[:, 0:NT, 1], ALU.subtract))
            link(dve.tensor_copy(parts[:, 0:NT, 2], w_rest))
            dve.wait_ge(consts, 7)

            dve.engine_nop().then_inc(compared, 2 * GI)
            for n, (first, end) in enumerate(zip(KEY_CHUNKS[:-1], KEY_CHUNKS[1:])):
                dve.wait_ge(loads[f"key{n}"], 16)
                with dve.Fori(0, end - first) as i:
                    t0 = i * (2 * GI) + first * (2 * GI)
                    dve.wait_ge(compared, t0 + 2 * GI)
                    for j in range(2 * GI):
                        width = P * (2 - j % 2)
                        dve.scalar_tensor_tensor(
                            out=junk[:, j, 0:width], in0=G[:, bass.ds((t0 + j) * P, width)],
                            scalar=keyT[:, bass.ds(t0 + j, 1)], in1=later_mask[:, 0:width],
                            op0=ALU.is_equal, op1=ALU.mult,
                            accum_out=later[:, bass.ds(t0 + j, 1)]).then_inc(compared, 1)
                if end % (NI // 4):
                    continue
                c = end // (NI // 4) - 1
                if c == 0:
                    dve.wait_ge(base_spread, 1)
                    link(dve.tensor_copy(base_bc, bank[3][:, 2 * P:2 * P + NG]))
                    dve.tensor_tensor(dstrel.rearrange("p (g j) -> p g j", j=2),
                                      dstT[:, 0:NT].rearrange("p (g j) -> p g j", j=2),
                                      base_bc.rearrange("p (g j) -> p g j", j=1).broadcast_to([P, NG, 2]),
                                      ALU.subtract).then_inc(dst_relative, 1)
                wait_emptied(dve, (("QT", "KT", "V", "V")[c], NB - 1))
                dve.wait_ge(dst_relative, 1)
                windows(dve, c)
                done = slice(c * NT // 4, (c + 1) * NT // 4)
                dve.wait_ge(compared, (c + 1) * NT // 4 + 2 * GI)
                link(dve.tensor_scalar(later[:, done], later[:, done], 0.0, None, ALU.is_equal))
                now = parts[:, done, :]
                dve.tensor_tensor(now, now, later[:, done].rearrange("p (t k) -> p t k", k=1).broadcast_to(
                    [P, NT // 4, 3]), ALU.mult).then_inc(flags_done, 1)
            dve.wait_ge(flags_done, 4)
            dve.wait_ge(windows_ready, 4)
            weights(dve, 3, rhs_dve)
            dve.wait_ge(diag_set, NB)
            dve.wait_ge(zeroed, 3)
            dve.wait_ge(rhs_pool, 3)
            dve.wait_ge(rhs_dve, 1)

            def renew(t, q):
                for j in range(1 + q // (GI - 1)):
                    dve.tensor_scalar(oh[:, q, j, :], iota_n[:, :], srcT[:, bass.ds(t + j, 1)], None, ALU.is_equal)
                dve.tensor_copy(rhs_now[:, q, :, :, :], rhs[:, bass.ds(t, 2), :, :]).then_inc(renewed, 1)

            for q in range(GI):
                renew(2 * q, q)
            dve.engine_nop().then_inc(group_folded, GI)

            def window_start(word, q):
                return dve.snap((((word >> (7 * q)) & 127) * 4).with_bounds(min_val=0, max_val=N - WIN))

            def clear(g, q, base):
                win = W_SD[:, :, bass.ds(base, WIN)]
                dve.wait_ge(count_ready, g + 1)
                dve.wait_ge(group_folded, g + GI)
                dve.scalar_tensor_tensor(out=win, in0=cnt_g[:, q, :, :], scalar=0.0, in1=win,
                                         op0=ALU.is_equal, op1=ALU.mult).then_inc(bias_cleared, 1)
                return win

            def fold(g, t_next, q, win):
                dve.wait_ge(bias_cleared, g + 1)
                dve.tensor_tensor(win, win, group_bank[q][:, :, 1, :], ALU.add).then_inc(group_folded, 1)
                renew(t_next, q)

            wide = dve.value_load(wide_i[0:1, 0:1], min_val=0, max_val=1)
            with dve.If(wide < 1):
                with dve.Fori(0, NI // 2) as ii:
                    for k in range(2 * GI):
                        if k == 0:
                            word = dve.value_load(packed_i[0:1, bass.ds(ii * 2, 1)], min_val=0, max_val=(1 << 28) - 1)
                            base = window_start(word, 0)
                        g = ii * (2 * GI) + k
                        win = clear(g, k % GI, base)
                        if k + 1 == GI:
                            word = dve.value_load(packed_i[0:1, bass.ds(ii * 2 + 1, 1)], min_val=0,
                                                  max_val=(1 << 28) - 1)
                        if k + 1 < 2 * GI:
                            base = window_start(word, (k + 1) % GI)
                        fold(g, ii * (4 * GI) + (2 * GI + 2 * k), k % GI, win)
            with dve.Else():
                dve.tensor_copy(dstrel, dstT[:, 0:NT]).then_inc(rebuild_step, 1)
                with dve.Fori(0, NWIN) as w:
                    dve.wait_ge(rebuild_step, w * 3 + 1)
                    windows(dve, None, rebuild_step)
                    dve.wait_ge(rebuild_step, w * 3 + 2)
                    weights(dve, None, rebuild_step)
                    for q in range(GI):
                        dve.wait_ge(rebuild_step, w * 3 + 3)
                        dve.tensor_copy(rhs_now[:, q, :, :, :], rhs[:, 2 * q:2 * q + 2, :, :]).then_inc(renewed, 1)
                    with dve.Fori(0, NI) as i:
                        for q in range(GI):
                            g = w * NG + i * GI + q
                            fold(g, (i + 1) * (2 * GI) + 2 * q, q, clear(g, q, w * WIN))
                    dve.tensor_scalar(dstrel, dstrel, float(WIN), None, ALU.subtract).then_inc(rebuild_step, 1)
            dve.engine_nop().then_inc(bias_built, 1)
            for b in range(NB):
                wait_full(dve, ("BD", b))
                dve.tensor_copy(B_DS[:, b, :], bank_of(("BD", b))[:, :]).then_inc(dve_emptied, 1)
            dve.wait_ge(dve_emptied, EMPTIED[("BD", NB - 1)][1])

            def row_least(h, b):
                k = h * NB + b
                dve.tensor_tensor_reduce(out=probs[:, k, :], in0=probs[:, k, :], in1=B_DS[:, b, :],
                                         scale=-1.0, scalar=3.0e38, op0=ALU.add, op1=ALU.min,
                                         accum_out=nmax[:, k:k + 1]).then_inc(row_max, 1)

            wait_emptied(dve, ("S", H - 1, NB - 1))
            for b in range(NB):
                row_least(0, b)
            for h in range(H):
                for b in range(NB):
                    if h + 1 < H:
                        row_least(h + 1, b)
                    if b % 2:
                        if b == 1 and h >= 2:
                            dve.wait_ge(head_done, h - 1)
                        wait_full(dve, ("PT", h, b))
                        dve.tensor_copy(probsT[h % 2][:, :, b * P:(b + 1) * P],
                                        bank_of(("PT", h, b))[:, :].rearrange("p (k n) -> p k n", k=NB)
                                        ).then_inc(dve_emptied, 1)
                if h == 1:
                    dve.wait_ge(count_built, 1)
                    dve.tensor_reduce(cnt_s[:, :], A_SD[:, :, :], AX.X, ALU.add).then_inc(degree_ready, 1)
                    wait_emptied(dve, ("AD", NB - 1))
                    dve.tensor_reduce(cnt_d[:, :], A_DS[:, :, :], AX.X, ALU.add).then_inc(degree_ready, 1)
                    dve.wait_ge(degree_ready, 2)
                    link(dve.reciprocal(rc[:, 0, :], cnt_s[:, :]))
                    link(dve.tensor_scalar(cnt_d[:, :], cnt_d[:, :], 1.0, None, ALU.max))
                    link(dve.reciprocal(rc[:, 1, :], cnt_d[:, :]))
            dve.wait_ge(exp_done, H * NB)
            link(dve.reciprocal(inverse_sums[:, :], row_sums[:, :]))
            by_row = inverse_sums[:, :].rearrange("p (h b) -> p b h", b=NB)
            for b in range(NB):
                dve.wait_ge(out_full, b + 1)
                dve.tensor_tensor(HH[:, b, :].rearrange("p (h d) -> p h d", h=H),
                                  bank[b][:, :].rearrange("p (h d) -> p h d", h=H),
                                  by_row[:, b, :].rearrange("p (h d) -> p h d", d=1).broadcast_to([P, H, HD]),
                                  ALU.mult).then_inc(out_taken, 1)

            n_ln = [0]

            def stats(z):
                k = n_ln[0] % 2
                link(dve.bn_stats(st[:, k, 0:6], z))
                dve.bn_aggr(mv[:, k, :], st[:, k, 0:6]).then_inc(stats_ready, 1)
                dve.wait_ge(std_ready, n_ln[0] + 1)
                link(dve.reciprocal(rstd[:, k, :], sd[:, k, :]))
                n_ln[0] += 1
                return mv[:, k, 0:1], rstd[:, k, :]

            def norm(dst, z, done):
                mu, r = stats(z)
                dve.tensor_scalar(dst, z, mu, r, ALU.subtract, ALU.mult).then_inc(done, 1)

            def norm_affine(dst, z, gain, shift, after):
                mu, r = stats(z)
                link(dve.scalar_tensor_tensor(out=z, in0=z, scalar=mu, in1=vec[:, slot[gain], :],
                                              op0=ALU.subtract, op1=ALU.mult))
                return dve.scalar_tensor_tensor(out=dst, in0=z, scalar=r, in1=shift, op0=ALU.mult, op1=ALU.add)

            def take(name, dst, resid):
                wait_full(dve, name)
                dve.tensor_tensor(dst, bank_of(name)[:, :], resid, ALU.add).then_inc(dve_emptied, 1)
                wait_emptied(dve, name)

            def take_scaled(name, dst, scale, resid):
                wait_full(dve, name)
                dve.scalar_tensor_tensor(out=dst, in0=bank_of(name)[:, :], scalar=scale, in1=resid, op0=ALU.mult,
                                         op1=ALU.add).then_inc(dve_emptied, 1)
                wait_emptied(dve, name)

            for v in ("g10", "be10", "g20"):
                dve.wait_ge(loads[v], 16)
            for b in range(NB):
                dve.wait_ge(resid_ready, b + 1)
                take(("WO", b), HH[:, b, :], RB[:, b, :])
                norm_affine(HH[:, b, :], HH[:, b, :], "g10", vec[:, slot["be10"], :], None).then_inc(h_ready, 1)
            for b in range(NB):
                dve.wait_ge(resid_ready, 2 * NB + b + 1)
                take(("W1", b), HH[:, b, :], RB[:, b, :])
                link(norm_affine(X[:, b, :], HH[:, b, :], "g20", QB[:, b, :], None))
                norm(X[:, b, :], X[:, b, :], x_ready)
            for b in range(NB):
                dve.wait_ge(resid_ready, 3 * NB + b + 1)
                take(("ALPHA", b), RB[:, b, :], RB[:, b, :])
            for b in range(NB):
                take_scaled(("SUM", b), HH[:, b, :], rc[:, 0, b:b + 1], RB[:, b, :])
                norm(X[:, b, :], HH[:, b, :], x_ready)
            dve.wait_ge(loads["bv2"], 16)

            def values2(b):
                wait_full(dve, ("V2", b))
                dve.tensor_tensor(VB[:, b, :], bank_of(("V2", b))[:, :], vec[:, slot["bv2"], :],
                                  ALU.add).then_inc(dve_emptied, 1)

            values2(0)

            def edges_of(u):
                return A_DS[:, u // 2, u % 2 * UN:(u % 2 + 1) * UN]

            def center(u):
                x = sT[:, u % 4, :, :]
                if u:
                    dve.wait_ge(centered, u)
                wait_emptied(dve, ("ST", u, H // 2 - 1))
                link(dve.tensor_tensor(max_tree[:, :, :], x[:, 0:4, :], x[:, 4:8, :], ALU.max))
                link(dve.tensor_tensor(max_tree[:, 0:2, :], max_tree[:, 0:2, :], max_tree[:, 2:4, :], ALU.max))
                link(dve.tensor_tensor(max_tree[:, 0, :], max_tree[:, 0, :], max_tree[:, 1, :], ALU.max))
                dve.tensor_tensor(x, x, max_tree[:, 0:1, :].broadcast_to([P, H, UN]),
                                  ALU.subtract).then_inc(centered, 1)

            def weigh(u):
                e = sT[:, u % 4, :, :]
                dve.wait_ge(inverse_ready, u + 1)
                link(dve.scalar_tensor_tensor(out=share, in0=edges_of(u), scalar=0.0, in1=sum_tree[:, u % 2, 3, :],
                                              op0=ALU.is_gt, op1=ALU.mult))
                dve.tensor_tensor(e, e, share.rearrange("p (h n) -> p h n", h=1).broadcast_to([P, H, UN]),
                                  ALU.mult).then_inc(soft_ready, 1)
                dve.wait_ge(soft_ready, u + 1)

            for u in range(NU):
                if u == NU - 1:
                    weigh(u - 2)
                center(u)
                if u < NB - 1:
                    values2(u + 1)
                if 2 <= u < NU - 1:
                    weigh(u - 2)
            weigh(NU - 2)
            weigh(NU - 1)
            for v in ("g12", "be12", "g22"):
                dve.wait_ge(loads[v], 16)
            for b in range(NB):
                dve.wait_ge(resid_ready, 4 * NB + b + 1)
                take(("WO2", b), HH[:, b, :], RB[:, b, :])
                norm_affine(HH[:, b, :], HH[:, b, :], "g12", vec[:, slot["be12"], :], None).then_inc(h_ready, 1)
            for b in range(NB):
                dve.wait_ge(resid_ready, 6 * NB + b + 1)
                take(("FF", b), HH[:, b, :], RB[:, b, :])
                link(norm_affine(X[:, b, :], HH[:, b, :], "g22", VB[:, b, :], None))
                norm(X[:, b, :], X[:, b, :], x_ready)
            for b in range(NB):
                dve.wait_ge(resid_ready, 7 * NB + b + 1)
                take(("Z1", b), RB[:, b, :], RB[:, b, :])
            for b in range(NB):
                take_scaled(("Z2", b), HH[:, b, :], rc[:, 1, b:b + 1], RB[:, b, :])
                norm(HH[:, b, :], HH[:, b, :], h_ready)

        @block.tensor
        def _(pe):
            def claim(name):
                k = POS[name]
                if k >= R:
                    wait_emptied(pe, ORDER[k - R][0])
                return bank_of(name)

            def product(name, lhs, rhs_, n_k=NB):
                t = claim(name)
                for k in range(n_k):
                    last = nc.tensor.matmul(t[:, :], lhs(k), rhs_(k), start=(k == 0), stop=(k == n_k - 1))
                last.then_inc(ring_full, 1)

            def turn(name, block_of):
                t = claim(name)
                for k in range(NB):
                    last = nc.tensor.transpose(t[:, k * P:(k + 1) * P], block_of(k), ident[:, :])
                last.then_inc(ring_full, 1)

            def cols(t, k, b):
                return t[:, k, b * P:(b + 1) * P]

            pe.wait_ge(consts, 7)
            pe.wait_ge(tile_ranges, 2)
            for k in range(2):
                last = nc.tensor.matmul(bank[3][0:1, k * P:(k + 1) * P], mm[:, k:k + 1], ident[:, :], start=True,
                                        stop=True)
            last.then_inc(ranges_turned, 1)
            pe.wait_ge(loads["ew"], 16)
            for k in range(4):
                last = nc.tensor.transpose(bank[2][:, k * P:(k + 1) * P], nat[:, k, :], ident[:, :])
            last.then_inc(edges_turned, 1)
            for k in range(NB):
                pe.wait_ge(loads[f"xT_{k}"], 16)
                pe.wait_ge(loads[f"wq0_{k}"], 16)
                for b in range(NB):
                    t = claim(("QT", b))
                    last = nc.tensor.matmul(t[:, :], cols(WA[:, 0, :, :], k, b), XT[:, k, :], start=(k == 0),
                                            stop=(k == NB - 1))
                    if k == NB - 1:
                        last.then_inc(ring_full, 1)
            pe.wait_ge(base_ready, 1)
            nc.tensor.matmul(bank[3][:, 2 * P:2 * P + NG], ones_row[:, :], base_row[:, 0:NG], start=True,
                             stop=True).then_inc(base_spread, 1)
            pe.wait_ge(loads["wk0"], 16)
            for b in range(NB):
                product(("KT", b), lambda k: cols(WA[:, 1, :, :], k, b), lambda k: XT[:, k, :])
            pe.wait_ge(loads["wv0"], 16)
            for b in range(NB):
                product(("V", b), lambda k: cols(XT, k, b), lambda k: WA[:, 2, k, :])
            wait_emptied(pe, ("KT", NB - 1))
            for h in range(H):
                r = slice((h % 2) * HD, (h % 2 + 1) * HD)
                for b in range(NB):
                    nc.tensor.matmul(claim(("S", h, b))[:, :], QB[r, h // 2, b * P:(b + 1) * P], KB[r, h // 2, :],
                                     start=True, stop=True).then_inc(ring_full, 1)

            def group(g, set_, q):
                pe.wait_ge(renewed, set_)
                if q < GI - 1:
                    pe.wait_ge(onehot_act, g + 1)
                pe.wait_ge(group_folded, g + 1)
                gb = group_bank[q]
                for b in range(NB):
                    for j in range(2):
                        src1 = oh[:, q, j, b * P:(b + 1) * P]
                        nc.tensor.matmul(gb[:, b, :, :], src1, rhs_now[:, q, j, 0:2, :], start=(j == 0), stop=False)
                        nc.tensor.matmul(gb[:, b, 1, :], src1, rhs_now[:, q, j, 2, :], start=False, stop=False)
                        last = nc.tensor.matmul(gb[:, b, 1, :], src1, rhs_now[:, q, j, 3, :], start=False,
                                                stop=(j == 1))
                last.then_inc(group_full, 1)

            wide = pe.value_load(wide_i[0:1, 0:1], min_val=0, max_val=1)
            with pe.If(wide < 1):
                with pe.Fori(0, NG, GI) as g0:
                    g0 = g0.with_bounds(max_val=NG - GI)
                    for q in range(GI):
                        group(g0 + q, g0 + q + 1, q)
            with pe.Else():
                with pe.Fori(0, NWIN) as w:
                    with pe.Fori(0, NG, GI) as g0:
                        g0 = g0.with_bounds(max_val=NG - GI)
                        for q in range(GI):
                            group(w * NG + g0 + q, w * (NG + GI) + g0 + (GI + q + 1), q)

            pe.wait_ge(bias_built, 1)
            for b in range(NB):
                turn(("BD", b), lambda k: cols(W_SD, k, b))
            pe.wait_ge(count_built, 1)
            for b in range(NB):
                turn(("AD", b), lambda k: cols(A_SD, k, b))

            pe.wait_ge(values_ready, NB)
            for h in range(H + 1):
                if h < H:
                    for b in range(NB):
                        pe.wait_ge(exp_done, h * NB + b + 1)
                        turn(("PT", h, b), lambda k: cols(probs, h * NB + b, k))
                if h == 0:
                    continue
                g = h - 1
                wait_emptied(pe, ("PT", g, NB - 2))
                wait_emptied(pe, ("PT", g, NB - 1))
                for b in range(NB):
                    for m in range(NB):
                        last = nc.tensor.matmul(bank[b][:, g * HD:(g + 1) * HD],
                                                probsT[g % 2][:, m, b * P:(b + 1) * P],
                                                VB[:, m, g * HD:(g + 1) * HD], start=(m == 0), stop=(m == NB - 1))
                    if g == H - 1:
                        last.then_inc(out_full, 1)
                if g < H - 1:
                    last.then_inc(head_done, 1)
            for b in range(NB):
                pe.wait_ge(out_taken, b + 1)
                turn(("OT", b), lambda k: cols(HH, b, k))
            pe.wait_ge(loads["wo0"], 16)
            for b in range(NB):
                wait_emptied(pe, ("OT", b))
                product(("WO", b), lambda k: cols(XT, k, b), lambda k: WB[:, k, :])
            pe.wait_ge(loads["w10"], 16)
            for b in range(NB + 1):
                if b < NB:
                    pe.wait_ge(h_ready, b + 1)
                    turn(("HT", b), lambda k: cols(HH, b, k))
                if b:
                    wait_emptied(pe, ("HT", b - 1))
                    product(("W1", b - 1), lambda k: cols(XT, k, b - 1), lambda k: WC[:, k, :])
            pe.wait_ge(loads["wcn"], 32)
            for b in range(NB + 1):
                if b < NB:
                    pe.wait_ge(x_ready, b + 1)
                    turn(("X1T", b), lambda k: cols(X, b, k))
                if b:
                    wait_emptied(pe, ("X1T", b - 1))
                    product(("BETA", b - 1), lambda k: cols(XT, k, b - 1), lambda k: wcn[:, 1, k, :])
                    product(("ALPHA", b - 1), lambda k: cols(XT, k, b - 1), lambda k: wcn[:, 0, k, :])
            wait_emptied(pe, ("BETA", NB - 1))
            for b in range(NB):
                product(("SUM", b), lambda k: cols(A_DS, k, b), lambda k: KB[:, k, :])
            def values2(b):
                wait_emptied(pe, ("X2T", b))
                product(("V2", b), lambda k: cols(XT, k, b), lambda k: WC[:, k, :])

            pe.wait_ge(loads["wqk2"], 32)
            pe.wait_ge(loads["wv2"], 16)
            for b in range(NB):
                pe.wait_ge(x_ready, NB + b + 1)
                turn(("X2T", b), lambda k: cols(X, b, k))
                if b == 2:
                    values2(0)
            wait_emptied(pe, ("X2T", NB - 1))
            for b in range(NB):
                product(("KT2", b), lambda k: cols(wqk2[:, 1, :, :], k, b), lambda k: XT[:, k, :])
            for b in range(NB):
                product(("QT2", b), lambda k: cols(wqk2[:, 0, :, :], k, b), lambda k: XT[:, k, :])
            def others_out(u):
                wait_emptied(pe, ("V2", u // 2))
                pe.wait_ge(notadj_ready, u // 2 + 1)
                for b in (u % 2 * 2, u % 2 * 2 + 1):
                    nc.tensor.matmul(bank[b][:, :], cols(NADJ, u // 2, b), VB[:, u // 2, :], start=(u < 2),
                                     stop=False, skip_group_check=True)

            def heads_out(u):
                m = u // 2
                pe.wait_ge(soft_ready, u + 1)
                for j in range(2):
                    for i, h in enumerate(UNIT_HEADS):
                        last = nc.tensor.matmul(bank[u % 2 * 2 + j][:, h * HD:(h + 1) * HD],
                                                sT[:, u % 4, i, j * P:(j + 1) * P],
                                                VB[:, m, h * HD:(h + 1) * HD], start=False, stop=(m == NB - 1),
                                                skip_group_check=True)
                    if m == NB - 1:
                        last.then_inc(out_full, 1)
                if m < NB - 1:
                    last.then_inc(head_done, 1)

            wait_emptied(pe, ("KT2", NB - 1))
            wait_emptied(pe, ("QT2", NB - 1))
            for u in range(NU + 3):
                if u < NU:
                    m, n = u // 2, slice(u % 2 * UN, (u % 2 + 1) * UN)
                    for p in range(H // 2):
                        t = claim(("ST", u, p))
                        for i, h in enumerate(UNIT_HEADS[2 * p:2 * p + 2]):
                            r = slice((h % 2) * HD, (h % 2 + 1) * HD)
                            last = nc.tensor.matmul(t[:, i * UN:(i + 1) * UN], KB[r, h // 2, m * P:(m + 1) * P],
                                                    QB[r, h // 2, n], start=True, stop=True)
                        last.then_inc(ring_full, 1)
                if u < NB - 1:
                    values2(u + 1)
                if u < NU:
                    others_out(u)
                if u >= 3:
                    heads_out(u - 3)
            for b in range(NB):
                pe.wait_ge(out_taken, NB + b + 1)
                turn(("OT2", b), lambda k: cols(HH, b, k))
            pe.wait_ge(loads["wo2"], 16)
            for b in range(NB):
                wait_emptied(pe, ("OT2", b))
                product(("WO2", b), lambda k: cols(XT, k, b), lambda k: WB[:, k, :])
            for b in range(NB):
                pe.wait_ge(h_ready, NB + b + 1)
                turn(("HT2", b), lambda k: cols(HH, b, k))
            wait_emptied(pe, ("HT2", NB - 1))
            pe.wait_ge(loads["w12a"], 16)
            pe.wait_ge(loads["w12b"], 16)
            for f in range(2 * NB):
                w1 = WC if f < NB else W_SD
                product(("FT", f), lambda k: cols(w1, k, f % NB), lambda k: XT[:, k, :])
            wait_emptied(pe, ("FT", 2 * NB - 1))
            pe.wait_ge(loads["w22"], 16)
            for b in range(NB):
                product(("FF", b), lambda k: cols(FT, k, b), lambda k: w22[:, k, :], n_k=2 * NB)
            pe.wait_ge(loads["w3a"], 16)
            for b in range(NB + 1):
                if b < NB:
                    pe.wait_ge(x_ready, 2 * NB + b + 1)
                    turn(("X3T", b), lambda k: cols(X, b, k))
                if b:
                    wait_emptied(pe, ("X3T", b - 1))
                    product(("Z1", b - 1), lambda k: cols(XT, k, b - 1), lambda k: WA[:, 1, k, :])
            for b in range(NB):
                product(("NST", b), lambda k: cols(X, k, b), lambda k: A_SD[:, k, :])
            wait_emptied(pe, ("NST", NB - 1))
            pe.wait_ge(loads["w3b"], 16)
            for b in range(NB):
                product(("Z2", b), lambda k: cols(QB, k, b), lambda k: WA[:, 2, k, :])


def kernel(x, src, dst, edge_weight, L0_gnn_Wqkv, L0_gnn_bqkv, L0_gnn_Wo, L0_gnn_bo, L0_gnn_W1, L0_gnn_b1,
           L0_gnn_g1, L0_gnn_beta1, L0_gnn_g2, L0_gnn_beta2, L1_gnn_wc, L1_gnn_wn, L1_gnn_bias, L2_gnn_Wq,
           L2_gnn_bq, L2_gnn_Wk, L2_gnn_bk, L2_gnn_Wv, L2_gnn_bv, L2_gnn_Wo, L2_gnn_bo, L2_gnn_W1, L2_gnn_b1,
           L2_gnn_W2, L2_gnn_b2, L2_gnn_g1, L2_gnn_be1, L2_gnn_g2, L2_gnn_be2, L3_gnn_W, L3_gnn_b):
    import numpy as np
    import concourse.bacc as bacc
    from concourse.bass_utils import run_bass_kernel_spmd

    def turned(w):
        return np.ascontiguousarray(np.asarray(w).T)

    arrays = {
        "x": x, "xT": turned(x), "src": src, "dst": dst, "ew": edge_weight,
        "wqkv0": turned(L0_gnn_Wqkv), "bqkv0": L0_gnn_bqkv, "wo0": turned(L0_gnn_Wo), "bo0": L0_gnn_bo,
        "w10": turned(L0_gnn_W1), "b10": L0_gnn_b1, "g10": L0_gnn_g1, "be10": L0_gnn_beta1, "g20": L0_gnn_g2,
        "be20": L0_gnn_beta2, "wc": L1_gnn_wc, "wn": L1_gnn_wn, "bias1": L1_gnn_bias,
        "wq2": L2_gnn_Wq, "wk2": L2_gnn_Wk, "wv2": L2_gnn_Wv,
        "bv2": L2_gnn_bv, "wo2": L2_gnn_Wo, "bo2": L2_gnn_bo, "w12": L2_gnn_W1,
        "w22": L2_gnn_W2, "b22": L2_gnn_b2, "g12": L2_gnn_g1, "be12": L2_gnn_be1, "g22": L2_gnn_g2,
        "be22": L2_gnn_be2, "w3": turned(L3_gnn_W), "b3": L3_gnn_b,
    }
    per_feature = [np.asarray(v).reshape(-1, P).T for v in
                   (np.asarray(L0_gnn_bqkv)[:2 * D], L2_gnn_bq, L2_gnn_bk, L2_gnn_b1)]
    arrays["cols"] = np.concatenate(per_feature, axis=1)
    arrays = {f"in_{k}": np.ascontiguousarray(v) for k, v in arrays.items()}
    nc = bacc.Bacc("TRN2", target_bir_lowering=False, num_devices=1)
    aps = {k[3:]: nc.dram_tensor(k, v.shape, mybir.dt.from_np(v.dtype), kind="ExternalInput").ap()
           for k, v in arrays.items()}
    out = nc.dram_tensor("out_x", (N, D), FP32, kind="ExternalOutput").ap()
    gnn_program(nc, aps, out)
    r = run_bass_kernel_spmd(nc, [arrays], core_ids=[0])
    return r.results[0]["out_x"]
```
